# Optimizing a Trainium2 kernel written in Bass

```python
import numpy as np
import jax
import jax.numpy as jnp

def _softmax(x, axis=-1):
    return jax.nn.softmax(x, axis=axis)

def _gelu(x):
    return jax.nn.gelu(x, approximate=True)

def _silu(x):
    return jax.nn.silu(x)

def _sigmoid(x):
    return jax.nn.sigmoid(x)

def _layernorm(x, axis=-1, eps=1e-05):
    m = jnp.mean(x, axis=axis, keepdims=True)
    v = jnp.var(x, axis=axis, keepdims=True)
    return (x - m) / jnp.sqrt(v + eps)

def _scatter_add(tgt, idx, src, axis=0):
    return tgt.at[idx].add(src)

def _segment_sum(src, seg, n):
    return jax.ops.segment_sum(src, seg, n)
kernel_name = 'mk_gnn_resnorm_d1_gnn_r32_bd027d'

def setup_inputs(seed: int=0):
    np.random.seed(seed)
    _w = jnp.asarray

    def _rec_inputs():
        import jax
        import jax.numpy as jnp
        _gk = jax.random.key(seed)
        x = -0.000202 + 1 * jax.random.normal(jax.random.fold_in(_gk, 1), (50000, 128), jnp.float32)
        _s = jax.random.randint(jax.random.fold_in(_gk, 2), (12500,), 0, 50000, jnp.int32)
        _d = jax.random.randint(jax.random.fold_in(_gk, 3), (12500,), 0, 50000, jnp.int32)
        _loop = jnp.arange(50000, dtype=jnp.int32)
        src = jnp.concatenate([_s, _d, _loop])
        dst = jnp.concatenate([_d, _s, _loop])
        _o = jnp.argsort(dst, stable=True)
        src = src[_o]
        dst = dst[_o]
        return (x, src, dst)
    x, src, dst = _rec_inputs()

    def _L0_gnn_setup():
        import jax, jax.numpy as jnp
        import numpy as np
        NUM_LAYERS = 4
        HIDDEN = 128
        N_NODES = 50000
        N_EDGES = 25000

        def _gru_cell(inp, h, w_ih, w_hh, b_ih, b_hh):
            gi = inp @ w_ih.T + b_ih
            gh = h @ w_hh.T + b_hh
            i_r, i_z, i_n = jnp.split(gi, 3, axis=-1)
            h_r, h_z, h_n = jnp.split(gh, 3, axis=-1)
            r = jax.nn.sigmoid(i_r + h_r)
            z = jax.nn.sigmoid(i_z + h_z)
            n = jnp.tanh(i_n + r * h_n)
            return (1.0 - z) * n + z * h
        key = jax.random.key(seed)
        ks = jax.random.split(key, 8)
        s = 1.0 / np.sqrt(HIDDEN)
        node_embed = jax.random.normal(ks[0], (N_NODES, HIDDEN), dtype=jnp.float32)
        edge_index = jax.random.randint(ks[1], (2, N_EDGES), 0, N_NODES, dtype=jnp.int64)
        weight = jax.random.normal(ks[2], (NUM_LAYERS, HIDDEN, HIDDEN), dtype=jnp.float32) * s
        w_ih = jax.random.normal(ks[3], (3 * HIDDEN, HIDDEN), dtype=jnp.float32) * s
        w_hh = jax.random.normal(ks[4], (3 * HIDDEN, HIDDEN), dtype=jnp.float32) * s
        b_ih = jax.random.normal(ks[5], (3 * HIDDEN,), dtype=jnp.float32) * s
        b_hh = jax.random.normal(ks[6], (3 * HIDDEN,), dtype=jnp.float32) * s
        return {'node_embed': node_embed, 'edge_index': edge_index, 'weight': weight, 'w_ih': w_ih, 'w_hh': w_hh, 'b_ih': b_ih, 'b_hh': b_hh}
    _L0_gnn_all = _L0_gnn_setup()
    _L0_gnn_in = {k: v for k, v in _L0_gnn_all.items() if k in ('weight', 'w_ih', 'w_hh', 'b_ih', 'b_hh')}
    del _L0_gnn_all
    return {'x': x, 'src': src, 'dst': dst, 'L0_gnn_weight': _L0_gnn_in['weight'], 'L0_gnn_w_ih': _L0_gnn_in['w_ih'], 'L0_gnn_w_hh': _L0_gnn_in['w_hh'], 'L0_gnn_b_ih': _L0_gnn_in['b_ih'], 'L0_gnn_b_hh': _L0_gnn_in['b_hh']}

def reference(x, src, dst, L0_gnn_weight, L0_gnn_w_ih, L0_gnn_w_hh, L0_gnn_b_ih, L0_gnn_b_hh):
    import jax
    import jax.numpy as jnp

    def _L0_gnn_ref(node_embed, edge_index, weight, w_ih, w_hh, b_ih, b_hh):
        import jax, jax.numpy as jnp
        import numpy as np
        NUM_LAYERS = 4
        HIDDEN = 128
        N_NODES = 50000
        N_EDGES = 25000

        def _gru_cell(inp, h, w_ih, w_hh, b_ih, b_hh):
            gi = inp @ w_ih.T + b_ih
            gh = h @ w_hh.T + b_hh
            i_r, i_z, i_n = jnp.split(gi, 3, axis=-1)
            h_r, h_z, h_n = jnp.split(gh, 3, axis=-1)
            r = jax.nn.sigmoid(i_r + h_r)
            z = jax.nn.sigmoid(i_z + h_z)
            n = jnp.tanh(i_n + r * h_n)
            return (1.0 - z) * n + z * h
        src = edge_index[0]
        dst = edge_index[1]
        n_nodes = node_embed.shape[0]
        x = node_embed
        for l in range(NUM_LAYERS):
            m = x @ weight[l]
            agg = jax.ops.segment_sum(m[src], dst, num_segments=n_nodes)
            x = _gru_cell(agg, x, w_ih, w_hh, b_ih, b_hh)
        return x + node_embed
    edge_index = jnp.stack([src, dst])
    x = _layernorm(x + _L0_gnn_ref(x, edge_index, L0_gnn_weight, L0_gnn_w_ih, L0_gnn_w_hh, L0_gnn_b_ih, L0_gnn_b_hh), axis=-1)
    return x

_drawn_inputs = setup_inputs


def setup_inputs(seed=0):
    import zlib

    import numpy as np

    out = dict(_drawn_inputs(seed))
    spreads = {}
    factors = {}
    for name, (base, spread) in spreads.items():
        noise = np.random.default_rng([zlib.crc32(name.encode()), seed]).standard_normal(out[name].shape)
        drawn = base * np.exp(spread * noise) if base else spread * noise
        out[name] = jnp.asarray(drawn.astype(out[name].dtype))
    for name, factor in factors.items():
        out[name] = (out[name] * factor).astype(out[name].dtype)
    return out
```

```python
from contextlib import ExitStack

import concourse.bass as bass
from concourse import mybir

F32 = mybir.dt.float32
I32 = mybir.dt.int32
ALU = mybir.AluOpType
ACT = mybir.ActivationFunctionType

P = 128
D = 128
ROWS = 80
RPP = 5
BLK = ROWS * RPP
TILES = 2
CAP = TILES * P
RING = 5
CHUNK = 120
WCH = 7
WIN = CHUNK * WCH
EPS = 1e-5

V_DIAG = 2
V_ROWS = 10
V_BIAS = 11
V_SLOTS = V_BIAS + 9 + 2 * (CAP // 8) - 1 + 3
V_TABLES = V_SLOTS + 1
V_CHECKS = V_TABLES + 3
V_FLAG = V_CHECKS + 1


def build(nc, x, src, dst, weight, w_ih, w_hh, b_ih, b_hh, out):
    N = x.shape[0]
    E = src.shape[0]
    L = weight.shape[0]
    NB = N // BLK
    GROUPS = NB // RING
    EP = NB
    EC = E // EP
    CPR = EC // CHUNK
    NCH = E // CHUNK
    assert NB * BLK == N and GROUPS * RING == NB and EP * EC == E and CPR * CHUNK == EC and NB <= P

    edge_sum = nc.dram_tensor("edge_sum", [N, D], F32, kind="Internal").ap()
    states = [x] + [nc.dram_tensor(f"state_{l}", [N, D], F32, kind="Internal").ap() for l in range(1, L)]

    def rows_of(t, b):
        v = t.rearrange("(b p k) f -> b p (k f)", p=ROWS, k=RPP)
        return v[bass.ds(b, 1), :, :].rearrange("b p m -> (b p) m")

    ctx = ExitStack()
    with ctx:
        def sb(name, shape, dt=F32):
            return ctx.enter_context(nc.sbuf_tensor(name, shape, dt))

        def ps(name, cols):
            return ctx.enter_context(nc.psum_tensor(name, [P, cols], F32))

        def sem(name):
            return ctx.enter_context(nc.semaphore(name))

        ident = sb("ident", [P, P])
        ones = sb("ones", [P, P])
        node_of_col = sb("node_of_col", [P, BLK])
        blk_start = sb("blk_start", [P, 1])
        w_in = sb("w_in", [P, L, D])
        wT = sb("wT", [P, L, D])
        wih_in = sb("wih_in", [P, 3, D])
        whh_in = sb("whh_in", [P, 3, D])
        wihT = sb("wihT", [P, 3 * D])
        whhT = sb("whhT", [P, 3 * D])
        wf = sb("wf", [P, L, 3 * D])
        bih = sb("bih", [P, 3])
        bhh = sb("bhh", [P, 3])
        bsum = sb("bsum", [P, 3])
        dst_i = sb("dst_i", [P, EC], I32)
        nxt_i = sb("nxt_i", [P, EC], I32)
        src_i = sb("src_i", [P, EC], I32)
        win_dst = sb("win_dst", [P, WIN + 1], I32)
        win_src = sb("win_src", [P, WIN], I32)
        winf = sb("winf", [P, WIN + 1])
        tmp_a = sb("tmp_a", [P, WIN])
        tmp_b = sb("tmp_b", [P, WIN])
        tmp_c = sb("tmp_c", [P, WIN])
        dl_i = sb("dl_i", [P, WIN], I32)
        key_i = sb("key_i", [P, WIN], I32)
        diag = sb("diag", [P, CPR, P])
        stat = sb("stat", [P, 8])
        sums = sb("sums", [P, 8])
        chunk_i = sb("chunk_i", [P, WCH], I32)
        keys = sb("keys", [P, CAP])
        slot_dl_i = sb("slot_dl_i", [P, CAP], I32)
        slot_src_i = sb("slot_src_i", [P, CAP], I32)
        slot_ok_i = sb("slot_ok_i", [P, CAP], I32)
        slot_dl = sb("slot_dl", [P, CAP])
        slot_src = sb("slot_src", [P, CAP])
        edge_dl = sb("edge_dl", [P, TILES, NB])
        edge_src = sb("edge_src", [P, TILES, NB], I32)
        idx = sb("idx", [P, TILES, RING], I32)
        checks = sb("checks", [P, 1])
        flag_i = sb("flag_i", [1, 1], I32)
        before = sb("before", [CHUNK, CHUNK])
        e_src = sb("e_src", [CHUNK, 1], I32)
        e_dst = sb("e_dst", [CHUNK, 1], I32)
        e_dstf = sb("e_dstf", [CHUNK, 1])
        e_diag = sb("e_diag", [CHUNK, CHUNK])
        e_same = sb("e_same", [CHUNK, CHUNK])
        e_junk = sb("e_junk", [CHUNK, CHUNK])
        e_dup = sb("e_dup", [CHUNK, 1])
        e_at = sb("e_at", [CHUNK, 1], I32)
        e_rows = sb("e_rows", [CHUNK, D])
        e_old = sb("e_old", [CHUNK, D])
        e_new = sb("e_new", [CHUNK, D])
        zeros = sb("zeros", [ROWS, RPP * D])
        h_rows = sb("h_rows", [ROWS, RING, RPP * D])
        gath = sb("gath", [P, RING, TILES, D])
        sel = sb("sel", [P, RING, TILES, BLK])
        hT = sb("hT", [P, RING, BLK])
        aggT = sb("aggT", [P, RING, BLK])
        rg = sb("rg", [P, RING, BLK])
        zg = sb("zg", [P, RING, BLK])
        ng = sb("ng", [P, RING, BLK])
        t1 = sb("t1", [P, RING, BLK])
        t2 = sb("t2", [P, RING, BLK])
        newT = sb("newT", [P, RING, BLK])
        o_rows = sb("o_rows", [ROWS, RING, RPP * D])
        x_rows = sb("x_rows", [ROWS, RING, RPP * D])
        y_rows = sb("y_rows", [ROWS, RING, RPP * D])
        bn = sb("bn", [ROWS, RING, RPP, 6])
        mv = sb("mv", [ROWS, RING, RPP, 4])
        veps = sb("veps", [ROWS, RING, RPP])
        rstd = sb("rstd", [ROWS, RING, RPP])
        nmr = sb("nmr", [ROWS, RING, RPP])
        mhalf = sb("mhalf", [ROWS, RPP])

        pH = ps("pH", 512)
        pA = ps("pA", 512)
        pR = ps("pR", 512)
        pZ = ps("pZ", 512)
        pHN = ps("pHN", 512)
        pIN = ps("pIN", 512)
        pO = ps("pO", 1024)

        s_w = sem("weights_loaded")
        s_edges = sem("edges_loaded")
        s_const = sem("constants_made")
        s_wt = sem("weight_transposes_done")
        s_wtc = sem("weight_transposes_copied")
        s_wf = sem("fused_weights_done")
        s_wfc = sem("fused_weights_copied")
        s_v = sem("vector_setup_steps")
        s_bc = sem("row_firsts_broadcast")
        s_win = sem("windows_gathered")
        s_tab = sem("tables_transposed")
        s_load = [sem(f"rows_loaded_{u}") for u in range(RING)]
        s_xld = [sem(f"x_rows_loaded_{u}") for u in range(RING)]
        s_gath = [sem(f"edges_gathered_{u}") for u in range(RING)]
        s_store = [sem(f"rows_stored_{u}") for u in range(RING)]
        s_pH = sem("h_transposed")
        s_hT = sem("h_copied")
        s_sel = sem("selection_built")
        s_pA = sem("edges_summed")
        s_agg = sem("agg_made")
        s_R = sem("r_product")
        s_Z = sem("z_product")
        s_HN = sem("hn_product")
        s_IN = sem("in_product")
        s_r = sem("r_gate")
        s_z = sem("z_gate")
        s_n = sem("n_gate")
        s_t1 = sem("r_times_hn")
        s_t2 = sem("n_argument")
        s_d = sem("h_minus_n")
        s_e = sem("z_times_difference")
        s_new = sem("new_state")
        s_pO = sem("state_transposed_back")
        s_o = sem("rows_ready")
        s_y = sem("residual_added")
        s_bn = sem("row_stats")
        s_mv = sem("row_moments")
        s_eps = sem("variance_plus_eps")
        s_rstd = sem("rstd_made")
        s_nmr = sem("shift_made")
        s_zero = sem("gather_buffers_cleared")
        s_idx = sem("block_indices_copied")

        s_flag = sem("checks_added_up")
        s_sum0 = sem("edge_sum_cleared")
        s_eld = sem("edge_row_loaded")
        s_ego = sem("edge_row_gathered")
        s_ediag = sem("destinations_on_diagonal")
        s_ebc = sem("destinations_broadcast")
        s_esum = sem("edge_row_summed")
        s_ev = sem("edge_row_vector_steps")
        s_esc = sem("edge_row_scattered")
        s_agld = sem("edge_sums_loaded")

        block = ctx.enter_context(nc.Block())

        def blocks(eng, step):
            for u in range(RING):
                step(0, u, u == 0, False)
            with eng.Fori(1, GROUPS - 1) as i:
                for u in range(RING):
                    step(i, u, False, False)
            for u in range(RING):
                step(GROUPS - 1, u, False, u == RING - 1)

        def after(i, u, k=1):
            i, u = i + (u + k) // RING, (u + k) % RING
            return RING * i + u, u, i

        def one_by_one(eng, step):
            step(0, True)
            with eng.Fori(1, NB) as b:
                step(b, False)

        @block.sync
        def _(sp):
            sp.dma_start(dst_i[0:EP, :], dst.rearrange("(p j) -> p j", p=EP)).then_inc(s_edges, 16)
            sp.dma_start(src_i[0:EP, :], src.rearrange("(p j) -> p j", p=EP)).then_inc(s_edges, 16)
            sp.wait_ge(s_const, 1)
            sp.dma_start(nxt_i[0:EP - 1, :],
                         dst[1:1 + (EP - 1) * EC].rearrange("(p j) -> p j", j=EC)).then_inc(s_edges, 16)
            sp.dma_start(nxt_i[EP - 1:EP, 0:EC - 1],
                         dst[1 + (EP - 1) * EC:E].rearrange("(p j) -> p j", p=1)).then_inc(s_edges, 16)
            sp.dma_start(w_in[:, :, :], weight.rearrange("l i o -> i l o")).then_inc(s_w, 16)
            sp.dma_start(wih_in[:, :, :], w_ih.rearrange("(c o) k -> o c k", c=3)).then_inc(s_w, 16)
            sp.dma_start(whh_in[:, :, :], w_hh.rearrange("(c o) k -> o c k", c=3)).then_inc(s_w, 16)
            sp.dma_start(bih[:, :], b_ih.rearrange("(c o) -> o c", c=3), allow_slow_non_contiguous=True).then_inc(s_w, 16)
            sp.dma_start(bhh[:, :], b_hh.rearrange("(c o) -> o c", c=3), allow_slow_non_contiguous=True).then_inc(s_w, 16)

            def load(l, b, u):
                sp.dma_start(h_rows[:, u, :], rows_of(states[l], b)).then_inc(s_load[u], 16)
                if l == L - 1:
                    sp.dma_start(x_rows[:, u, :], rows_of(x, b)).then_inc(s_xld[u], 16)

            def store(l, b, u):
                sp.wait_ge(s_o, l * NB + b + 1)
                to = out if l == L - 1 else states[l + 1]
                sp.dma_start(rows_of(to, b), o_rows[:, u, :]).then_inc(s_store[u], 16)

            def fast_path():
                for l in range(L):
                    if l:
                        for u in range(RING):
                            sp.wait_ge(s_store[u], 16 * GROUPS * l)
                        sp.wait_ge(s_pH, l * NB)
                    for u in range(RING):
                        load(l, u, u)
                    with sp.Fori(0, GROUPS - 1) as i:
                        for u in range(RING):
                            b = RING * i + u
                            store(l, b, u)
                            load(l, b + RING, u)
                    for u in range(RING):
                        store(l, NB - RING + u, u)
                for u in range(RING):
                    sp.wait_ge(s_store[u], 16 * GROUPS * L)

            def general_path():
                for l in range(L):
                    if l:
                        sp.wait_ge(s_store[0], 16 * NB * l)
                    with sp.Fori(0, NB) as b:
                        sp.dma_start(rows_of(edge_sum, b), zeros[:, :]).then_inc(s_sum0, 16)
                    sp.wait_ge(s_sum0, 16 * NB * (l + 1))

                    def edge_row(r, first):
                        if not (first and l == 0):
                            sp.wait_ge(s_esc, 16 * (l * NCH + r))
                            sp.nop(nofuse=True)
                        for arr, to in ((src, e_src), (dst, e_dst)):
                            rows = arr.rearrange("(r j o) -> r j o", j=CHUNK, o=1)
                            sp.dma_start(to[:, :], rows[bass.ds(r, 1), :, :].rearrange("r j o -> (r j) o")).then_inc(s_eld, 16)

                    edge_row(0, True)
                    with sp.Fori(1, NCH) as r:
                        edge_row(r, False)
                    sp.wait_ge(s_esc, 16 * NCH * (l + 1))

                    def one(b, first):
                        if not (first and l == 0):
                            sp.wait_ge(s_store[0], 16 * (l * NB + b))
                            sp.nop(nofuse=True)
                        load(l, b, 0)
                        sp.dma_start(y_rows[:, 1, :], rows_of(edge_sum, b)).then_inc(s_agld, 16)
                        store(l, b, 0)

                    one_by_one(sp, one)
                sp.wait_ge(s_store[0], 16 * NB * L)

            sp.wait_ge(s_v, V_FLAG)
            flag = sp.value_load(flag_i[0:1, 0:1])
            with sp.If(flag == 0):
                fast_path()
            with sp.Else():
                general_path()

        @block.gpsimd
        def _(pool):
            nc.gpsimd.memset(nxt_i[:, :], N).then_inc(s_const, 1)
            nc.gpsimd.memset(ones[:, :], 1.0).then_inc(s_const, 1)
            nc.gpsimd.memset(ident[:, :], 0.0).then_inc(s_zero, 1)
            nc.gpsimd.iota(node_of_col[:, :], [[1, RPP], [RPP, ROWS]], base=0, channel_multiplier=0,
                           allow_small_or_imprecise_dtypes=True).then_inc(s_const, 1)
            nc.gpsimd.iota(blk_start[:, :], [[0, 1]], base=0, channel_multiplier=BLK,
                           allow_small_or_imprecise_dtypes=True).then_inc(s_const, 1)
            pool.wait_ge(s_zero, 1)
            nc.gpsimd.affine_select(out=ident[:, :], in_=ident[:, :], compare_op=ALU.not_equal, fill=1.0, base=0,
                                    pattern=[[-1, P]], channel_multiplier=1).then_inc(s_const, 1)
            nc.gpsimd.memset(win_dst[:, :], -1).then_inc(s_zero, 1)
            nc.gpsimd.memset(win_src[:, :], 0).then_inc(s_zero, 1)
            nc.gpsimd.memset(gath[:, :, :, :], 0.0).then_inc(s_zero, 1)
            nc.gpsimd.memset(mhalf[:, :], -0.5).then_inc(s_zero, 1)
            nc.gpsimd.memset(zeros[:, :], 0.0).then_inc(s_zero, 1)
            nc.gpsimd.memset(before[:, :], 1.0).then_inc(s_zero, 1)
            pool.wait_ge(s_zero, 7)
            nc.gpsimd.affine_select(out=before[:, :], in_=before[:, :], compare_op=ALU.is_gt, fill=0.0, base=0,
                                    pattern=[[-1, CHUNK]], channel_multiplier=1).then_inc(s_zero, 1)
            pool.wait_ge(s_v, V_ROWS)
            for m in range(WCH):
                for arr, win in ((dst, win_dst), (src, win_src)):
                    pool.indirect_dma_start(
                        out=win[0:NB, m * CHUNK:(m + 1) * CHUNK], out_offset=None,
                        in_=arr.rearrange("(r j) -> r j", j=CHUNK),
                        in_offset=bass.IndirectOffsetOnAxis(ap=chunk_i[0:NB, m:m + 1], axis=0),
                        bounds_check=NCH - 1, oob_is_err=False).then_inc(s_win, 16)

            last_node = pool.to_reg(N - 1)

            def root(l, b, u):
                pool.wait_ge(s_eps, b + 1)
                nc.gpsimd.tensor_tensor(rstd[:, u, :], veps[:, u, :], mhalf[:, :], ALU.pow).then_inc(s_rstd, 1)

            def fast_path():
                for l in range(L):
                    if l:
                        for u in range(RING):
                            pool.wait_ge(s_store[u], 16 * GROUPS * l)

                    def gather(b, u, used):
                        g = l * NB + b
                        if used:
                            pool.wait_ge(s_pA, g - RING + 1)
                            pool.nop(nofuse=True)
                        nc.gpsimd.tensor_copy(idx[:, :, u:u + 1], edge_src[:, :, bass.ds(b, 1)]).then_inc(s_idx, 1)
                        pool.wait_ge(s_idx, g + 1)
                        pool.nop(nofuse=True)
                        for j in range(TILES):
                            pool.indirect_dma_start(
                                out=gath[:, u, j, :], out_offset=None, in_=states[l],
                                in_offset=bass.IndirectOffsetOnAxis(ap=idx[:, j, u:u + 1], axis=0),
                                bounds_check=last_node, oob_is_err=False).then_inc(s_gath[u], 16)

                    for u in range(RING):
                        gather(u, u, l > 0)
                    with pool.Fori(1, GROUPS) as i:
                        for u in range(RING):
                            gather(RING * i + u, u, True)
                            if l == L - 1:
                                root(l, RING * (i - 1) + u, u)
                    if l == L - 1:
                        for u in range(RING):
                            root(l, NB - RING + u, u)

            def general_path():
                for l in range(L):
                    def edge_row(r, first):
                        k = l * NCH + r
                        pool.wait_ge(s_eld, 2 * 16 * (k + 1))
                        pool.nop(nofuse=True)
                        for frm, at, to in ((states[l], e_src, e_rows), (edge_sum, e_dst, e_old)):
                            pool.indirect_dma_start(out=to[:, :], out_offset=None, in_=frm,
                                                    in_offset=bass.IndirectOffsetOnAxis(ap=at[:, :], axis=0),
                                                    bounds_check=last_node, oob_is_err=False).then_inc(s_ego, 16)
                        pool.wait_ge(s_ev, 5 * (k + 1))
                        pool.nop(nofuse=True)
                        pool.indirect_dma_start(out=edge_sum, in_=e_new[:, :], in_offset=None,
                                                out_offset=bass.IndirectOffsetOnAxis(ap=e_at[:, :], axis=0),
                                                bounds_check=last_node, oob_is_err=False).then_inc(s_esc, 16)

                    edge_row(0, True)
                    with pool.Fori(1, NCH) as r:
                        edge_row(r, False)
                one_by_one(pool, lambda b, first: root(L - 1, b, 0))

            pool.wait_ge(s_v, V_FLAG)
            flag = pool.value_load(flag_i[0:1, 0:1])
            with pool.If(flag == 0):
                fast_path()
            with pool.Else():
                general_path()

        @block.tensor
        def _(pe):
            pe.wait_ge(s_w, 5 * 16)
            pe.wait_ge(s_const, 5)
            for l in range(L):
                nc.tensor.transpose(pH[:, l * D:(l + 1) * D], w_in[:, l, :], ident[:, :])
            for c in range(3):
                nc.tensor.transpose(pA[:, c * D:(c + 1) * D], wih_in[:, c, :], ident[:, :])
            for c in range(3):
                last = nc.tensor.transpose(pR[:, c * D:(c + 1) * D], whh_in[:, c, :], ident[:, :])
            last.then_inc(s_wt, 1)
            pe.wait_ge(s_wtc, 3)
            for l, bank in enumerate((pZ, pHN, pIN, pH)):
                nc.tensor.matmul(bank[:, 0:3 * D], wT[:, l, :], wihT[:, :], start=True, stop=True).then_inc(s_wf, 1)
            pe.wait_ge(s_v, V_DIAG)
            for m in range(CPR):
                c = m * P
                last = nc.tensor.matmul(pO[0:NB, c:c + EP], ones[0:EP, 0:NB], diag[0:EP, m, 0:EP], start=True, stop=True)
            last.then_inc(s_bc, 1)
            pe.wait_ge(s_v, V_SLOTS)
            for j in range(TILES):
                nc.tensor.transpose(pA[:, j * NB:(j + 1) * NB], slot_dl[0:NB, j * P:(j + 1) * P], ident[0:NB, 0:NB])
            for j in range(TILES):
                last = nc.tensor.transpose(pA[:, (TILES + j) * NB:(TILES + j + 1) * NB],
                                           slot_src[0:NB, j * P:(j + 1) * P], ident[0:NB, 0:NB])
            last.then_inc(s_tab, 1)
            pe.wait_ge(s_v, V_CHECKS)
            pe.wait_ge(s_wfc, L)
            nc.tensor.matmul(pR[0:1, 0:1], checks[0:NB, :], ones[0:NB, 0:1], start=True, stop=True).then_inc(s_flag, 1)

            def at_least(s, value, start):
                if not start:
                    pe.wait_ge(s, value)

            def turn_h(l, b, u, loads, start):
                g = l * NB + b
                pe.wait_ge(s_load[u], 16 * loads)
                at_least(s_hT, g, start)
                for k in range(RPP):
                    last = nc.tensor.transpose(pH[:, k * ROWS:(k + 1) * ROWS], h_rows[:, u, k * D:(k + 1) * D],
                                               ident[0:ROWS, 0:ROWS])
                last.then_inc(s_pH, 1)

            def sum_edges(l, b, u, gathers, start):
                g = l * NB + b
                pe.wait_ge(s_gath[u], 16 * TILES * gathers)
                pe.wait_ge(s_sel, g + 1)
                at_least(s_agg, g, start)
                for j in range(TILES):
                    last = nc.tensor.matmul(pA[:, 0:BLK], gath[:, u, j, :], sel[:, u, j, :],
                                            start=j == 0, stop=j == TILES - 1)
                last.then_inc(s_pA, 1)

            def gates(l, b, u, start):
                g = l * NB + b
                pe.wait_ge(s_hT, g + 1)
                pe.wait_ge(s_agg, g + 1)
                for bank, c, free, done in ((pR, 0, s_r, s_R), (pZ, 1, s_z, s_Z)):
                    at_least(free, g, start)
                    nc.tensor.matmul(bank[:, 0:BLK], wf[:, l, c * D:(c + 1) * D], aggT[:, u, :], start=True, stop=False)
                    nc.tensor.matmul(bank[:, 0:BLK], whhT[:, c * D:(c + 1) * D], hT[:, u, :],
                                     start=False, stop=True).then_inc(done, 1)
                at_least(s_t1, g, start)
                nc.tensor.matmul(pHN[:, 0:BLK], whhT[:, 2 * D:3 * D], hT[:, u, :], start=True, stop=True).then_inc(s_HN, 1)
                at_least(s_t2, g, start)
                nc.tensor.matmul(pIN[:, 0:BLK], wf[:, l, 2 * D:3 * D], aggT[:, u, :], start=True, stop=True).then_inc(s_IN, 1)

            def turn_back(l, b, u, start):
                g = l * NB + b
                pe.wait_ge(s_new, g + 1)
                if l == L - 1:
                    if start:
                        pe.wait_ge(s_o, l * NB)
                    else:
                        pe.wait_ge(s_y, b)
                else:
                    at_least(s_o, g, start and l == 0)
                for k in range(RPP):
                    last = nc.tensor.transpose(pO[0:ROWS, k * D:(k + 1) * D], newT[:, u, k * ROWS:(k + 1) * ROWS],
                                               ident[:, :])
                last.then_inc(s_pO, 1)

            def fast_path():
                for l in range(L):
                    def step(i, u, first, last):
                        start = first and l == 0
                        if first:
                            turn_h(l, 0, 0, GROUPS * l + 1, start)
                            sum_edges(l, 0, 0, GROUPS * l + 1, start)
                        if not last:
                            nb, nu, ni = after(i, u)
                            turn_h(l, nb, nu, GROUPS * l + ni + 1, False)
                            sum_edges(l, nb, nu, GROUPS * l + ni + 1, False)
                        gates(l, RING * i + u, u, start)
                        if not first:
                            pb, pu, _ = after(i, u, -1)
                            turn_back(l, pb, pu, isinstance(i, int) and pb == 0)
                        if last:
                            turn_back(l, RING * i + u, u, False)

                    blocks(pe, step)

            def general_path():
                for l in range(L):
                    def edge_row(r, first):
                        k = l * NCH + r
                        pe.wait_ge(s_ediag, k + 1)
                        nc.tensor.matmul(pZ[0:CHUNK, 0:CHUNK], ones[0:CHUNK, 0:CHUNK], e_diag[:, :],
                                         start=True, stop=True).then_inc(s_ebc, 1)
                        pe.wait_ge(s_ev, 5 * k + 2)
                        pe.wait_ge(s_ego, 2 * 16 * (k + 1))
                        nc.tensor.matmul(pHN[0:CHUNK, 0:D], e_same[:, :], e_rows[:, :],
                                         start=True, stop=True).then_inc(s_esum, 1)

                    edge_row(0, True)
                    with pe.Fori(1, NCH) as r:
                        edge_row(r, False)

                    def one(b, first):
                        start = first and l == 0
                        turn_h(l, b, 0, l * NB + b + 1, start)
                        pe.wait_ge(s_agld, 16 * (l * NB + b + 1))
                        at_least(s_agg, l * NB + b, start)
                        for k in range(RPP):
                            last = nc.tensor.transpose(pA[:, k * ROWS:(k + 1) * ROWS], y_rows[:, 1, k * D:(k + 1) * D],
                                                       ident[0:ROWS, 0:ROWS])
                        last.then_inc(s_pA, 1)
                        gates(l, b, 0, start)
                        turn_back(l, b, 0, first)

                    one_by_one(pe, one)

            pe.wait_ge(s_v, V_FLAG)
            flag = pe.value_load(flag_i[0:1, 0:1])
            with pe.If(flag == 0):
                fast_path()
            with pe.Else():
                general_path()

        @block.scalar
        def _(act):
            act.wait_ge(s_wt, 1)
            nc.scalar.copy(wT[:, :, :].rearrange("p l d -> p (l d)"), pH[:, 0:L * D]).then_inc(s_wtc, 1)
            nc.scalar.copy(wihT[:, :], pA[:, 0:3 * D]).then_inc(s_wtc, 1)
            nc.scalar.copy(whhT[:, :], pR[:, 0:3 * D]).then_inc(s_wtc, 1)
            for l, bank in enumerate((pZ, pHN, pIN, pH)):
                act.wait_ge(s_wf, l + 1)
                nc.scalar.copy(wf[:, l, :], bank[:, 0:3 * D]).then_inc(s_wfc, 1)

            def copy_h(l, b, u):
                act.wait_ge(s_pH, l * NB + b + 1)
                nc.scalar.copy(hT[:, u, :], pH[:, 0:BLK]).then_inc(s_hT, 1)

            def gates(l, b, u):
                g = l * NB + b
                act.wait_ge(s_R, g + 1)
                nc.scalar.activation(rg[:, u, :], pR[:, 0:BLK], ACT.Sigmoid, bias=bsum[:, 0:1]).then_inc(s_r, 1)
                act.wait_ge(s_Z, g + 1)
                nc.scalar.activation(zg[:, u, :], pZ[:, 0:BLK], ACT.Sigmoid, bias=bsum[:, 1:2]).then_inc(s_z, 1)
                act.wait_ge(s_t2, g + 1)
                nc.scalar.activation(ng[:, u, :], t2[:, u, :], ACT.Tanh, bias=bih[:, 2:3]).then_inc(s_n, 1)

            def rows_out(l, b, u, stored):
                g = l * NB + b
                if stored is not None:
                    act.wait_ge(s_store[u], 16 * stored)
                if l < L - 1:
                    act.wait_ge(s_pO, g + 1)
                    nc.scalar.copy(o_rows[:, u, :], pO[0:ROWS, 0:RPP * D]).then_inc(s_o, 1)
                else:
                    act.wait_ge(s_nmr, b + 1)
                    for k in range(RPP):
                        last = nc.scalar.activation(o_rows[:, u, k * D:(k + 1) * D], y_rows[:, u, k * D:(k + 1) * D],
                                                    ACT.Identity, bias=nmr[:, u, k:k + 1], scale=rstd[:, u, k:k + 1])
                    last.then_inc(s_o, 1)

            def fast_path():
                for l in range(L):
                    def earlier(i):
                        return None if l == 0 and isinstance(i, int) and i == 0 else GROUPS * l + i

                    def step(i, u, first, last):
                        if first:
                            copy_h(l, 0, 0)
                        if not last:
                            copy_h(l, *after(i, u)[:2])
                        gates(l, RING * i + u, u)
                        if not first:
                            pb, pu, pi = after(i, u, -1)
                            rows_out(l, pb, pu, earlier(pi))
                        if last:
                            rows_out(l, RING * i + u, u, earlier(i))

                    blocks(act, step)

            def general_path():
                for l in range(L):
                    def one(b, first):
                        copy_h(l, b, 0)
                        gates(l, b, 0)
                        rows_out(l, b, 0, None if first and l == 0 else l * NB + b)

                    one_by_one(act, one)

            act.wait_ge(s_v, V_FLAG)
            flag = act.value_load(flag_i[0:1, 0:1])
            with act.If(flag == 0):
                fast_path()
            with act.Else():
                general_path()

        @block.vector
        def _(dve):
            steps = [0]

            def done(ins):
                steps[0] += 1
                ins.then_inc(s_v, 1)
                dve.wait_ge(s_v, steps[0])

            v = nc.vector
            n_ = slice(0, NB)
            dve.wait_ge(s_edges, 4 * 16)
            dve.wait_ge(s_const, 5)
            firsts = dst_i[0:EP, :].rearrange("p (m j) -> p m j", j=CHUNK)[:, :, 0]
            done(v.tensor_copy(stat[0:EP, 0:CPR], firsts))
            for m in range(CPR):
                last = v.tensor_scalar(diag[0:EP, m, 0:EP], ident[0:EP, 0:EP], stat[0:EP, m:m + 1], None, ALU.mult)
            done(last)
            assert steps[0] == V_DIAG
            done(v.tensor_tensor(tmp_a[0:EP, 0:EC], nxt_i[0:EP, :], dst_i[0:EP, :], ALU.subtract))
            done(v.tensor_tensor(tmp_b[0:EP, 0:EC], src_i[0:EP, :], dst_i[0:EP, :], ALU.not_equal))
            done(v.scalar_tensor_tensor(tmp_c[0:EP, 0:EC], tmp_a[0:EP, 0:EC], 1.0, tmp_b[0:EP, 0:EC],
                                        ALU.is_equal, ALU.mult, accum_out=sums[0:EP, 0:1]))
            done(v.tensor_scalar(tmp_c[0:EP, 0:EC], tmp_a[0:EP, 0:EC], 0.0, None, ALU.is_equal, ALU.add,
                                 accum_out=sums[0:EP, 1:2]))
            done(v.tensor_scalar(tmp_c[0:EP, 0:EC], tmp_a[0:EP, 0:EC], 1.0, None, ALU.is_equal, ALU.add,
                                 accum_out=sums[0:EP, 2:3]))
            dve.wait_ge(s_bc, 1)
            bc = pO[n_, 0:CPR * P].rearrange("p (m q) -> p m q", q=P)[:, :, 0:EP]
            done(v.tensor_scalar(tmp_c[n_, 0:CPR * EP].rearrange("p (m q) -> p m q", q=EP), bc, blk_start[n_, :], None,
                                 ALU.is_lt, ALU.add, accum_out=stat[n_, 5:6]))
            done(v.tensor_scalar(stat[n_, 6:7], stat[n_, 5:6], -1.0, 0.0, ALU.add, ALU.max))
            for m in range(WCH):
                last = v.tensor_scalar(chunk_i[n_, m:m + 1], stat[n_, 6:7], float(m), None, ALU.add)
            done(last)
            assert steps[0] == V_ROWS
            dve.wait_ge(s_w, 5 * 16)
            done(v.tensor_tensor(bsum[:, :], bih[:, :], bhh[:, :], ALU.add))
            assert steps[0] == V_BIAS
            dve.wait_ge(s_win, 2 * WCH * 16)
            done(v.tensor_copy(winf[n_, :], win_dst[n_, :]))
            done(v.tensor_tensor(tmp_b[n_, :], winf[n_, 0:WIN], winf[n_, 1:WIN + 1], ALU.is_equal))
            done(v.tensor_scalar(tmp_a[n_, :], winf[n_, 0:WIN], blk_start[n_, :], None, ALU.subtract))
            done(v.scalar_tensor_tensor(tmp_c[n_, :], tmp_a[n_, :], 0.0, tmp_b[n_, :], ALU.is_ge, ALU.mult))
            done(v.scalar_tensor_tensor(tmp_b[n_, :], tmp_a[n_, :], float(BLK), tmp_c[n_, :], ALU.is_lt, ALU.mult,
                                        accum_out=sums[n_, 3:4]))
            done(v.tensor_scalar(dl_i[n_, :], tmp_a[n_, :], 0.0, float(BLK - 1), ALU.max, ALU.min))
            done(v.tensor_scalar(key_i[n_, :], dl_i[n_, :], 16, 1 << 30, ALU.logical_shift_left, ALU.bitwise_or))
            done(v.tensor_tensor(dl_i[n_, :], key_i[n_, :], win_src[n_, :], ALU.bitwise_or))
            done(v.tensor_tensor(tmp_a[n_, :], dl_i[n_, :].bitcast(F32), tmp_b[n_, :], ALU.mult))
            cur, nxt = tmp_a, tmp_c
            for r in range(CAP // 8):
                done(v.max(keys[n_, 8 * r:8 * r + 8], cur[n_, :]))
                if r < CAP // 8 - 1:
                    done(v.match_replace(nxt[n_, :], keys[n_, 8 * r:8 * r + 8], cur[n_, :], 0.0))
                    cur, nxt = nxt, cur
            ki = keys[n_, :].bitcast(I32)
            v.tensor_scalar(slot_dl_i[n_, :], ki, 16, None, ALU.logical_shift_right)
            v.tensor_scalar(slot_ok_i[n_, :], ki, 30, None, ALU.logical_shift_right)
            done(v.tensor_scalar(slot_src_i[n_, :], ki, 0xFFFF, None, ALU.bitwise_and))
            v.tensor_scalar(slot_dl[n_, :], slot_dl_i[n_, :], -16384.0, None, ALU.add)
            done(v.tensor_scalar(tmp_b[n_, 0:CAP], slot_ok_i[n_, :], -65536.0, 65536.0, ALU.mult, ALU.add))
            done(v.tensor_tensor(slot_src[n_, :], tmp_b[n_, 0:CAP], slot_src_i[n_, :], ALU.add))
            assert steps[0] == V_SLOTS
            dve.wait_ge(s_tab, 1)
            v.tensor_copy(edge_dl[:, :, :].rearrange("p j b -> p (j b)"), pA[:, 0:TILES * NB])
            done(v.tensor_copy(edge_src[:, :, :].rearrange("p j b -> p (j b)"), pA[:, TILES * NB:2 * TILES * NB]))
            assert steps[0] == V_TABLES
            done(v.tensor_tensor(checks[n_, :], sums[n_, 0:1], sums[n_, 1:2], ALU.subtract))
            done(v.scalar_tensor_tensor(checks[n_, :], checks[n_, :], float(EC), sums[n_, 2:3], ALU.add, ALU.subtract))
            done(v.scalar_tensor_tensor(checks[n_, :], sums[n_, 3:4], float(CAP), checks[n_, :], ALU.is_gt, ALU.add))
            assert steps[0] == V_CHECKS
            dve.wait_ge(s_flag, 1)
            done(v.tensor_tensor(flag_i[0:1, 0:1], pR[0:1, 0:1], dst_i[0:1, 0:1], ALU.add))
            assert steps[0] == V_FLAG

            def select(l, b, u):
                for j in range(TILES):
                    last = v.tensor_scalar(sel[:, u, j, :], node_of_col[:, :],
                                           edge_dl[:, j, bass.ds(b, 1)], None, ALU.is_equal)
                last.then_inc(s_sel, 1)

            def aggregate(l, b, u):
                g = l * NB + b
                dve.wait_ge(s_hT, g + 1)
                dve.wait_ge(s_pA, g + 1)
                v.tensor_tensor(aggT[:, u, :], pA[:, 0:BLK], hT[:, u, :], ALU.add).then_inc(s_agg, 1)

            def n_argument(l, b, u):
                g = l * NB + b
                dve.wait_ge(s_HN, g + 1)
                dve.wait_ge(s_r, g + 1)
                v.scalar_tensor_tensor(t1[:, u, :], pHN[:, 0:BLK], bhh[:, 2:3], rg[:, u, :],
                                       ALU.add, ALU.mult).then_inc(s_t1, 1)
                dve.wait_ge(s_IN, g + 1)
                dve.wait_ge(s_t1, g + 1)
                v.tensor_tensor(t2[:, u, :], pIN[:, 0:BLK], t1[:, u, :], ALU.add).then_inc(s_t2, 1)

            def mix(l, b, u):
                g = l * NB + b
                dve.wait_ge(s_n, g + 1)
                v.tensor_tensor(t1[:, u, :], hT[:, u, :], ng[:, u, :], ALU.subtract).then_inc(s_d, 1)
                dve.wait_ge(s_z, g + 1)
                dve.wait_ge(s_d, g + 1)
                v.tensor_tensor(t2[:, u, :], zg[:, u, :], t1[:, u, :], ALU.mult).then_inc(s_e, 1)
                dve.wait_ge(s_e, g + 1)
                v.tensor_tensor(newT[:, u, :], t2[:, u, :], ng[:, u, :], ALU.add).then_inc(s_new, 1)

            def normalise(l, b, u, loads):
                dve.wait_ge(s_pO, l * NB + b + 1)
                dve.wait_ge(s_xld[u], 16 * loads)
                v.scalar_tensor_tensor(y_rows[:, u, :], x_rows[:, u, :], 2.0, pO[0:ROWS, 0:RPP * D],
                                       ALU.mult, ALU.add).then_inc(s_y, 1)
                dve.wait_ge(s_y, b + 1)
                for k in range(RPP):
                    last = v.bn_stats(bn[:, u, k, :], y_rows[:, u, k * D:(k + 1) * D])
                last.then_inc(s_bn, 1)
                dve.wait_ge(s_bn, b + 1)
                v.tensor_tensor(mv[:, u, :, 0], bn[:, u, :, 1], bn[:, u, :, 4], ALU.add)
                v.scalar_tensor_tensor(mv[:, u, :, 1], bn[:, u, :, 2], D * EPS, bn[:, u, :, 5], ALU.add, ALU.add)
                v.tensor_tensor(mv[:, u, :, 2], bn[:, u, :, 1], bn[:, u, :, 4], ALU.subtract).then_inc(s_mv, 1)
                dve.wait_ge(s_mv, 2 * b + 1)
                v.scalar_tensor_tensor(mv[:, u, :, 3], mv[:, u, :, 2], 0.25, mv[:, u, :, 2],
                                       ALU.mult, ALU.mult).then_inc(s_mv, 1)
                dve.wait_ge(s_mv, 2 * b + 2)
                v.scalar_tensor_tensor(veps[:, u, :], mv[:, u, :, 1], 1.0 / D, mv[:, u, :, 3],
                                       ALU.mult, ALU.add).then_inc(s_eps, 1)
                dve.wait_ge(s_rstd, b + 1)
                v.scalar_tensor_tensor(nmr[:, u, :], mv[:, u, :, 0], -0.5, rstd[:, u, :],
                                       ALU.mult, ALU.mult).then_inc(s_nmr, 1)

            def fast_path():
                for l in range(L):
                    def step(i, u, first, last):
                        if first:
                            select(l, 0, 0)
                            aggregate(l, 0, 0)
                            select(l, 1, 1)
                        if not last:
                            aggregate(l, *after(i, u)[:2])
                        n_argument(l, RING * i + u, u)
                        if not (isinstance(i, int) and RING * i + u >= NB - 2):
                            select(l, *after(i, u, 2)[:2])
                        mix(l, RING * i + u, u)
                        if l == L - 1:
                            if not first:
                                pb, pu, pi = after(i, u, -1)
                                normalise(l, pb, pu, pi + 1)
                            if last:
                                normalise(l, RING * i + u, u, i + 1)

                    blocks(dve, step)

            def general_path():
                dve.wait_ge(s_zero, 8)
                for l in range(L):
                    def edge_row(r, first):
                        k = l * NCH + r
                        dve.wait_ge(s_eld, 2 * 16 * (k + 1))
                        v.tensor_copy(e_dstf[:, :], e_dst[:, :]).then_inc(s_ev, 1)
                        dve.wait_ge(s_ev, 5 * k + 1)
                        v.tensor_scalar(e_diag[:, :], ident[0:CHUNK, 0:CHUNK], e_dstf[:, :], None,
                                        ALU.mult).then_inc(s_ediag, 1)
                        dve.wait_ge(s_ebc, k + 1)
                        v.tensor_scalar(e_same[:, :], pZ[0:CHUNK, 0:CHUNK], e_dstf[:, :], None,
                                        ALU.is_equal).then_inc(s_ev, 1)
                        dve.wait_ge(s_ev, 5 * k + 2)
                        v.scalar_tensor_tensor(e_junk[:, :], e_same[:, :], 1.0, before[:, :], ALU.mult, ALU.mult,
                                               accum_out=e_dup[:, :]).then_inc(s_ev, 1)
                        dve.wait_ge(s_ev, 5 * k + 3)
                        v.scalar_tensor_tensor(e_at[:, :], e_dup[:, :], 65536.0, e_dstf[:, :],
                                               ALU.mult, ALU.add).then_inc(s_ev, 1)
                        dve.wait_ge(s_esum, k + 1)
                        v.tensor_tensor(e_new[:, :], pHN[0:CHUNK, 0:D], e_old[:, :], ALU.add).then_inc(s_ev, 1)

                    edge_row(0, True)
                    with dve.Fori(1, NCH) as r:
                        edge_row(r, False)

                    def one(b, first):
                        dve.wait_ge(s_pA, l * NB + b + 1)
                        v.tensor_copy(aggT[:, 0, :], pA[:, 0:BLK]).then_inc(s_agg, 1)
                        n_argument(l, b, 0)
                        mix(l, b, 0)
                        if l == L - 1:
                            normalise(l, b, 0, b + 1)

                    one_by_one(dve, one)

            flag = dve.value_load(flag_i[0:1, 0:1])
            with dve.If(flag == 0):
                fast_path()
            with dve.Else():
                general_path()


_INS = ['x', 'src', 'dst', 'L0_gnn_weight', 'L0_gnn_w_ih', 'L0_gnn_w_hh', 'L0_gnn_b_ih', 'L0_gnn_b_hh']
_OUTS = [((50000, 128), 'float32')]


def kernel(**inputs):
    import numpy as _np
    import concourse.bacc as _bacc
    from concourse import mybir as _mybir
    from concourse.bass_utils import run_bass_kernel_spmd as _run

    nc = _bacc.Bacc("TRN2", target_bir_lowering=False, num_devices=1)
    arrays, args = {}, []
    for name in _INS:
        a = _np.ascontiguousarray(inputs[name])
        arrays[f"in_{name}_dram"] = a
        args.append(nc.dram_tensor(f"in_{name}_dram", a.shape, _mybir.dt.from_np(a.dtype), kind="ExternalInput").ap())
    for i, (shape, dtype) in enumerate(_OUTS):
        dt = _mybir.dt.from_np(_np.dtype(dtype))
        args.append(nc.dram_tensor(f"out_{i}_dram", shape, dt, kind="ExternalOutput").ap())
    build(nc, *args)
    r = _run(nc, [arrays], core_ids=[0])
    got = tuple(r.results[0][f"out_{i}_dram"] for i in range(len(_OUTS)))
    return got[0]
```

```python
from contextlib import ExitStack

import concourse.bass as bass
from concourse import mybir

F32 = mybir.dt.float32
F32R = mybir.dt.float32r
I32 = mybir.dt.int32
ALU = mybir.AluOpType
ACT = mybir.ActivationFunctionType

P = 128
D = 128
ROWS = 100
RPP = 4
BLK = ROWS * RPP
TILES = 2
CAP = TILES * P
RING = 5
CHUNK = 120
WCH = 7
WIN = CHUNK * WCH
LIVE = CHUNK + BLK + CAP
SHRINK = 16
EPS = 1e-5
NLAG = 3

V_DIAG = 2
V_ROWS = 10
V_BIAS = V_ROWS + 8
V_WEIGHTS = V_BIAS + 1
V_SLOTS = V_WEIGHTS + 2 + 2 * (CAP // 8) - 1 + 4
V_TABLES = V_SLOTS + 1
V_CHECKS = V_TABLES + 3
V_FLAG = V_CHECKS + 1


def build(nc, x, src, dst, weight, w_ih, w_hh, b_ih, b_hh, out):
    N = x.shape[0]
    E = src.shape[0]
    L = weight.shape[0]
    NB = N // BLK
    GROUPS = NB // RING
    EP = NB
    EC = E // EP
    CPR = EC // CHUNK
    NCH = E // CHUNK
    assert NB * BLK == N and GROUPS * RING == NB and EP * EC == E and CPR * CHUNK == EC and NB <= P

    edge_sum = nc.dram_tensor("edge_sum", [N, D], F32, kind="Internal").ap()
    states = [x] + [nc.dram_tensor(f"state_{l}", [N, D], F32, kind="Internal").ap() for l in range(1, L)]

    def rows_of(t, b):
        v = t.rearrange("(b p k) f -> b p (k f)", p=ROWS, k=RPP)
        return v[bass.ds(b, 1), :, :].rearrange("b p m -> (b p) m")

    ctx = ExitStack()
    with ctx:
        def sb(name, shape, dt=F32):
            return ctx.enter_context(nc.sbuf_tensor(name, shape, dt))

        def ps(name, cols):
            return ctx.enter_context(nc.psum_tensor(name, [P, cols], F32))

        def sem(name):
            return ctx.enter_context(nc.semaphore(name))

        ident = sb("ident", [P, P])
        ones = sb("ones", [P, P])
        node_of_col = sb("node_of_col", [P, BLK])
        blk_start = sb("blk_start", [P, 1])
        w_in = sb("w_in", [P, L, D])
        wT = sb("wT", [P, L, D])
        wih_in = sb("wih_in", [P, 3, D])
        whh_in = sb("whh_in", [P, 3, D])
        wihT = sb("wihT", [P, 3 * D])
        whh_hi = sb("whh_hi", [P, 3 * D], F32R)
        whh_lo = sb("whh_lo", [P, 3 * D], F32R)
        wf_hi = sb("wf_hi", [P, L, 3 * D], F32R)
        wf_lo = sb("wf_lo", [P, L, 3 * D], F32R)
        bih = sb("bih", [P, 3])
        bhh = sb("bhh", [P, 3])
        bsum = sb("bsum", [P, 3])
        dst_i = sb("dst_i", [P, EC], I32)
        nxt_i = sb("nxt_i", [P, EC], I32)
        src_i = sb("src_i", [P, EC], I32)
        win_dst = sb("win_dst", [P, WIN + 1], I32)
        win_src = sb("win_src", [P, WIN], I32)
        winf = sb("winf", [P, WIN + 1])
        dl_i = sb("dl_i", [P, WIN], I32)
        diag = sb("diag", [P, CPR, P])
        stat = sb("stat", [P, 8])
        sums = sb("sums", [P, 8])
        chunk_i = sb("chunk_i", [P, WCH], I32)
        keys = sb("keys", [P, CAP])
        slot_dl_i = sb("slot_dl_i", [P, CAP], I32)
        slot_src_i = sb("slot_src_i", [P, CAP], I32)
        slot_ok_i = sb("slot_ok_i", [P, CAP], I32)
        slot_dl = sb("slot_dl", [P, CAP])
        slot_src = sb("slot_src", [P, CAP])
        edge_dl = sb("edge_dl", [P, TILES, NB])
        edge_src = sb("edge_src", [P, TILES, NB], I32)
        idx = sb("idx", [P, TILES, RING], I32)
        checks = sb("checks", [P, 1])
        flag_i = sb("flag_i", [1, 1], I32)
        before = sb("before", [CHUNK, CHUNK])
        e_src = sb("e_src", [CHUNK, 1], I32)
        e_dst = sb("e_dst", [CHUNK, 1], I32)
        e_dstf = sb("e_dstf", [CHUNK, 1])
        e_diag = sb("e_diag", [CHUNK, CHUNK])
        e_same = sb("e_same", [CHUNK, CHUNK])
        e_junk = sb("e_junk", [CHUNK, CHUNK])
        e_dup = sb("e_dup", [CHUNK, 1])
        e_at = sb("e_at", [CHUNK, 1], I32)
        e_rows = sb("e_rows", [CHUNK, D])
        e_old = sb("e_old", [CHUNK, D])
        e_new = sb("e_new", [CHUNK, D])
        zeros = sb("zeros", [ROWS, RPP * D])
        h_rows = sb("h_rows", [ROWS, RING, RPP * D])
        gath = sb("gath", [P, RING, TILES, D])
        g_hi = sb("g_hi", [P, RING, TILES, D], F32R)
        g_lo = sb("g_lo", [P, RING, TILES, D], F32R)
        sel = sb("sel", [P, RING, TILES, BLK], F32R)
        hT = sb("hT", [P, RING, BLK])
        h_hi = sb("h_hi", [P, RING, BLK], F32R)
        h_lo = sb("h_lo", [P, RING, BLK], F32R)
        aggT = sb("aggT", [P, RING, BLK])
        a_hi = sb("a_hi", [P, RING, BLK], F32R)
        a_lo = sb("a_lo", [P, RING, BLK], F32R)
        rg = sb("rg", [P, BLK])
        zg = sb("zg", [P, BLK])
        ng = sb("ng", [P, BLK])
        t1 = sb("t1", [P, BLK])
        t2 = sb("t2", [P, BLK])
        newT = sb("newT", [P, RING, BLK])
        new_flat = newT[:, :, :].rearrange("p r n -> p (r n)")
        h_flat = hT[:, :, :].rearrange("p r n -> p (r n)")
        tmp_a, tmp_b = new_flat[:, 0:WIN], new_flat[:, WIN:2 * WIN]
        tmp_c, key_i = h_flat[:, 0:WIN], h_flat[:, WIN:2 * WIN].bitcast(I32)
        o_rows = sb("o_rows", [ROWS, RING, RPP * D])
        x_rows = sb("x_rows", [ROWS, RING, RPP * D])
        y_rows = sb("y_rows", [ROWS, RING, RPP * D])
        bn = sb("bn", [ROWS, RING, RPP, 6])
        mv = sb("mv", [ROWS, RING, RPP, 4])
        veps = sb("veps", [ROWS, RING, RPP])
        rstd = sb("rstd", [ROWS, RING, RPP])
        nmr = sb("nmr", [ROWS, RING, RPP])
        mhalf = sb("mhalf", [ROWS, RPP])

        pH = ps("pH", 512)
        pA = ps("pA", 512)
        pR = ps("pR", 512)
        pZ = ps("pZ", 512)
        pHN = ps("pHN", 512)
        pIN = ps("pIN", 512)
        pO = ps("pO", 1024)

        s_w = sem("weights_loaded")
        s_edges = sem("edges_loaded")
        s_const = sem("constants_made")
        s_wt = sem("weight_transposes_done")
        s_wtc = sem("weight_transposes_copied")
        s_wf = sem("fused_weights_done")
        s_wfc = sem("fused_weights_copied")
        s_v = sem("vector_setup_steps")
        s_bc = sem("row_firsts_broadcast")
        s_win = sem("dst_windows_gathered")
        s_winsrc = sem("src_windows_gathered")
        s_tab = sem("tables_transposed")
        s_load = [sem(f"rows_loaded_{u}") for u in range(RING)]
        s_xld = [sem(f"x_rows_loaded_{u}") for u in range(RING)]
        s_gath = [sem(f"edges_gathered_{u}") for u in range(RING)]
        s_store = [sem(f"rows_stored_{u}") for u in range(RING)]
        s_pH = sem("h_transposed")
        s_hT = sem("h_copied")
        s_hhi = sem("h_high_parts")
        s_hlo = sem("h_low_parts")
        s_ghi = sem("gathered_high_parts")
        s_glo = sem("gathered_low_parts")
        s_ahi = sem("agg_high_parts")
        s_alo = sem("agg_low_parts")
        s_sel = sem("selection_built")
        s_pA = sem("edges_summed")
        s_agg = sem("agg_made")
        s_R = sem("r_product")
        s_Z = sem("z_product")
        s_HN = sem("hn_product")
        s_IN = sem("in_product")
        s_r = sem("r_gate")
        s_z = sem("z_gate")
        s_n = sem("n_gate")
        s_t1 = sem("r_times_hn")
        s_t2 = sem("n_argument")
        s_d = sem("h_minus_n")
        s_e = sem("z_times_difference")
        s_new = sem("new_state")
        s_pO = sem("state_transposed_back")
        s_o = sem("rows_ready")
        s_y = sem("residual_added")
        s_bn = sem("row_stats")
        s_mv = sem("row_moments")
        s_eps = sem("variance_plus_eps")
        s_rstd = sem("rstd_made")
        s_nmr = sem("shift_made")
        s_zero = sem("gather_buffers_cleared")
        s_idx = sem("block_indices_copied")

        s_flag = sem("checks_added_up")
        s_sum0 = sem("edge_sum_cleared")
        s_eld = [sem(f"edge_rows_loaded_{l}") for l in range(L)]
        s_ego = [sem(f"edge_rows_gathered_{l}") for l in range(L)]
        s_ediag = sem("destinations_on_diagonal")
        s_ebc = sem("destinations_broadcast")
        s_esum = sem("edge_row_summed")
        s_ev = sem("edge_row_vector_steps")
        s_esc = sem("edge_row_scattered")
        s_agld = sem("edge_sums_loaded")

        block = ctx.enter_context(nc.Block())

        def blocks(eng, step):
            for u in range(RING):
                step(0, u, u == 0, False)
            with eng.Fori(1, GROUPS - 1) as i:
                for u in range(RING):
                    step(i, u, False, False)
            for u in range(RING):
                step(GROUPS - 1, u, False, u == RING - 1)

        def after(i, u, k=1):
            i, u = i + (u + k) // RING, (u + k) % RING
            return RING * i + u, u, i

        def exists(i, u, k):
            return not isinstance(i, int) or RING * i + u + k < NB

        def exists_before(i, u, k):
            return not isinstance(i, int) or RING * i + u >= k

        def one_by_one(eng, step):
            step(0, True)
            with eng.Fori(1, NB) as b:
                step(b, False)

        @block.sync
        def _(sp):
            sp.dma_start(dst_i[0:EP, :], dst.rearrange("(p j) -> p j", p=EP)).then_inc(s_edges, 16)
            sp.dma_start(src_i[0:EP, :], src.rearrange("(p j) -> p j", p=EP)).then_inc(s_edges, 16)
            sp.wait_ge(s_const, 1)
            sp.dma_start(nxt_i[0:EP - 1, :],
                         dst[1:1 + (EP - 1) * EC].rearrange("(p j) -> p j", j=EC)).then_inc(s_edges, 16)
            sp.dma_start(nxt_i[EP - 1:EP, 0:EC - 1],
                         dst[1 + (EP - 1) * EC:E].rearrange("(p j) -> p j", p=1)).then_inc(s_edges, 16)
            sp.dma_start(w_in[:, :, :], weight.rearrange("l i o -> i l o")).then_inc(s_w, 16)
            sp.dma_start(wih_in[:, :, :], w_ih.rearrange("(c o) k -> o c k", c=3)).then_inc(s_w, 16)
            sp.dma_start(whh_in[:, :, :], w_hh.rearrange("(c o) k -> o c k", c=3)).then_inc(s_w, 16)
            sp.dma_start(bih[:, :], b_ih.rearrange("(c o) -> o c", c=3), allow_slow_non_contiguous=True).then_inc(s_w, 16)
            sp.dma_start(bhh[:, :], b_hh.rearrange("(c o) -> o c", c=3), allow_slow_non_contiguous=True).then_inc(s_w, 16)

            def load(l, b, u):
                sp.dma_start(h_rows[:, u, :], rows_of(states[l], b)).then_inc(s_load[u], 16)

            def load_x(b, u):
                sp.dma_start(x_rows[:, u, :], rows_of(x, b)).then_inc(s_xld[u], 16)

            def store(l, b, u):
                sp.wait_ge(s_o, l * NB + b + 1)
                to = out if l == L - 1 else states[l + 1]
                sp.dma_start(rows_of(to, b), o_rows[:, u, :]).then_inc(s_store[u], 16)

            def fast_path():
                for l in range(L):
                    if l:
                        for u in range(RING):
                            sp.wait_ge(s_store[u], 16 * GROUPS * l)
                        sp.wait_ge(s_pH, l * NB)
                    for u in range(RING):
                        load(l, u, u)
                    if l == L - 1:
                        for u in range(RING):
                            load_x(u, u)

                    def step(i, u, first, last):
                        if exists(i, u, RING):
                            sp.wait_ge(s_pH, l * NB + RING * i + u + 1)
                            sp.nop(nofuse=True)
                            load(l, RING * i + u + RING, u)
                        if l < L - 1:
                            store(l, RING * i + u, u)
                        elif exists_before(i, u, NLAG + 1):
                            pb, pu, _ = after(i, u, -NLAG - 1)
                            store(l, pb, pu)
                            if exists(i, u, RING - NLAG - 1):
                                load_x(pb + RING, pu)

                    blocks(sp, step)
                    if l == L - 1:
                        for k in range(NLAG + 1, 0, -1):
                            pb, pu, _ = after(GROUPS, 0, -k)
                            store(l, pb, pu)
                for u in range(RING):
                    sp.wait_ge(s_store[u], 16 * GROUPS * L)

            def general_path():
                for l in range(L):
                    if l:
                        sp.wait_ge(s_store[0], 16 * NB * l)
                    with sp.Fori(0, NB) as b:
                        sp.dma_start(rows_of(edge_sum, b), zeros[:, :]).then_inc(s_sum0, 16)
                    sp.wait_ge(s_sum0, 16 * NB * (l + 1))

                    def edge_row(r, first):
                        if not (first and l == 0):
                            sp.wait_ge(s_esc, 16 * (l * NCH + r))
                            sp.nop(nofuse=True)
                        for arr, to in ((src, e_src), (dst, e_dst)):
                            rows = arr.rearrange("(r j o) -> r j o", j=CHUNK, o=1)
                            sp.dma_start(to[:, :], rows[bass.ds(r, 1), :, :].rearrange("r j o -> (r j) o")).then_inc(s_eld[l], 16)

                    edge_row(0, True)
                    with sp.Fori(1, NCH) as r:
                        edge_row(r, False)
                    sp.wait_ge(s_esc, 16 * NCH * (l + 1))

                    def one(b, first):
                        if not (first and l == 0):
                            sp.wait_ge(s_store[0], 16 * (l * NB + b))
                            sp.nop(nofuse=True)
                        load(l, b, 0)
                        if l == L - 1:
                            load_x(b, 0)
                        sp.dma_start(y_rows[:, 1, :], rows_of(edge_sum, b)).then_inc(s_agld, 16)
                        store(l, b, 0)

                    one_by_one(sp, one)
                sp.wait_ge(s_store[0], 16 * NB * L)

            sp.wait_ge(s_v, V_FLAG)
            flag = sp.value_load(flag_i[0:1, 0:1])
            with sp.If(flag == 0):
                fast_path()
            with sp.Else():
                general_path()

        @block.gpsimd
        def _(pool):
            nc.gpsimd.memset(nxt_i[:, :], N).then_inc(s_const, 1)
            nc.gpsimd.memset(ones[:, :], 1.0).then_inc(s_const, 1)
            nc.gpsimd.memset(ident[:, :], 0.0).then_inc(s_zero, 1)
            nc.gpsimd.iota(node_of_col[:, :], [[1, RPP], [RPP, ROWS]], base=0, channel_multiplier=0,
                           allow_small_or_imprecise_dtypes=True).then_inc(s_const, 1)
            nc.gpsimd.iota(blk_start[:, :], [[0, 1]], base=0, channel_multiplier=BLK,
                           allow_small_or_imprecise_dtypes=True).then_inc(s_const, 1)
            pool.wait_ge(s_zero, 1)
            nc.gpsimd.affine_select(out=ident[:, :], in_=ident[:, :], compare_op=ALU.not_equal, fill=1.0, base=0,
                                    pattern=[[-1, P]], channel_multiplier=1).then_inc(s_const, 1)
            nc.gpsimd.memset(win_dst[:, :], -1).then_inc(s_zero, 1)
            nc.gpsimd.memset(win_src[:, :], 0).then_inc(s_zero, 1)
            nc.gpsimd.memset(gath[:, :, :, :], 0.0).then_inc(s_zero, 1)
            nc.gpsimd.memset(mhalf[:, :], -0.5).then_inc(s_zero, 1)
            nc.gpsimd.memset(zeros[:, :], 0.0).then_inc(s_zero, 1)
            nc.gpsimd.memset(before[:, :], 1.0).then_inc(s_zero, 1)
            pool.wait_ge(s_zero, 7)
            nc.gpsimd.affine_select(out=before[:, :], in_=before[:, :], compare_op=ALU.is_gt, fill=0.0, base=0,
                                    pattern=[[-1, CHUNK]], channel_multiplier=1).then_inc(s_zero, 1)
            pool.wait_ge(s_v, V_ROWS)
            for arr, win, arrived in ((dst, win_dst, s_win), (src, win_src, s_winsrc)):
                for m in range(WCH):
                    pool.indirect_dma_start(
                        out=win[0:NB, m * CHUNK:(m + 1) * CHUNK], out_offset=None,
                        in_=arr.rearrange("(r j) -> r j", j=CHUNK),
                        in_offset=bass.IndirectOffsetOnAxis(ap=chunk_i[0:NB, m:m + 1], axis=0),
                        bounds_check=NCH - 1, oob_is_err=False).then_inc(arrived, 16)

            last_node = pool.to_reg(N - 1)

            def split_h(l, b, u):
                pool.wait_ge(s_hhi, l * NB + b + 1)
                nc.gpsimd.tensor_tensor(h_lo[:, u, :], hT[:, u, :], h_hi[:, u, :].bitcast(F32),
                                        ALU.subtract).then_inc(s_hlo, 1)

            def root(b, u):
                pool.wait_ge(s_eps, b + 1)
                nc.gpsimd.tensor_tensor(rstd[:, u, :], veps[:, u, :], mhalf[:, :], ALU.pow).then_inc(s_rstd, 1)

            def fast_path():
                for l in range(L):
                    if l:
                        for u in range(RING):
                            pool.wait_ge(s_store[u], 16 * GROUPS * l)

                    def gather(b, u, used):
                        g = l * NB + b
                        if used:
                            pool.wait_ge(s_glo, g - RING + 1)
                            pool.nop(nofuse=True)
                        nc.gpsimd.tensor_copy(idx[:, :, u:u + 1], edge_src[:, :, bass.ds(b, 1)]).then_inc(s_idx, 1)
                        pool.wait_ge(s_idx, g + 1)
                        pool.nop(nofuse=True)
                        for j in range(TILES):
                            pool.indirect_dma_start(
                                out=gath[:, u, j, :], out_offset=None, in_=states[l],
                                in_offset=bass.IndirectOffsetOnAxis(ap=idx[:, j, u:u + 1], axis=0),
                                bounds_check=last_node, oob_is_err=False).then_inc(s_gath[u], 16)

                    def split_gathered(b, u):
                        pool.wait_ge(s_ghi, l * NB + b + 1)
                        nc.gpsimd.tensor_tensor(g_lo[:, u, :, :], gath[:, u, :, :], g_hi[:, u, :, :].bitcast(F32),
                                                ALU.subtract).then_inc(s_glo, 1)

                    def step(i, u, first, last):
                        if first:
                            gather(0, 0, l > 0)
                            for v in range(3):
                                gather(v + 1, v + 1, l > 0)
                                split_gathered(v, v)
                                if v < 2:
                                    split_h(l, v, v)
                        if exists(i, u, RING - 1):
                            nb, nu, ni = after(i, u, RING - 1)
                            gather(nb, nu, l > 0 or not isinstance(ni, int) or ni > 0)
                        if exists(i, u, 2):
                            split_h(l, *after(i, u, 2)[:2])
                        if exists(i, u, 3):
                            split_gathered(*after(i, u, 3)[:2])
                        if l == L - 1 and exists_before(i, u, NLAG):
                            root(*after(i, u, -NLAG)[:2])

                    blocks(pool, step)
                    if l == L - 1:
                        for k in range(NLAG, 0, -1):
                            root(*after(GROUPS, 0, -k)[:2])

            def general_path():
                for l in range(L):
                    def edge_row(r, first):
                        k = l * NCH + r
                        pool.wait_ge(s_eld[l], 2 * 16 * (r + 1))
                        pool.nop(nofuse=True)
                        for frm, at, to in ((states[l], e_src, e_rows), (edge_sum, e_dst, e_old)):
                            pool.indirect_dma_start(out=to[:, :], out_offset=None, in_=frm,
                                                    in_offset=bass.IndirectOffsetOnAxis(ap=at[:, :], axis=0),
                                                    bounds_check=last_node, oob_is_err=False).then_inc(s_ego[l], 16)
                        pool.wait_ge(s_ev, 5 * (k + 1))
                        pool.nop(nofuse=True)
                        pool.indirect_dma_start(out=edge_sum, in_=e_new[:, :], in_offset=None,
                                                out_offset=bass.IndirectOffsetOnAxis(ap=e_at[:, :], axis=0),
                                                bounds_check=last_node, oob_is_err=False).then_inc(s_esc, 16)

                    edge_row(0, True)
                    with pool.Fori(1, NCH) as r:
                        edge_row(r, False)

                    def one(b, first):
                        split_h(l, b, 0)
                        if l == L - 1:
                            root(b, 0)

                    one_by_one(pool, one)

            pool.wait_ge(s_v, V_FLAG)
            flag = pool.value_load(flag_i[0:1, 0:1])
            with pool.If(flag == 0):
                fast_path()
            with pool.Else():
                general_path()

        @block.tensor
        def _(pe):
            pe.wait_ge(s_const, 5)
            pe.wait_ge(s_v, V_DIAG)
            for m in range(CPR):
                c = m * P
                last = nc.tensor.matmul(pO[0:NB, c:c + EP], ones[0:EP, 0:NB], diag[0:EP, m, 0:EP], start=True, stop=True)
            last.then_inc(s_bc, 1)
            pe.wait_ge(s_w, 5 * 16)
            for l in range(L):
                nc.tensor.transpose(pH[:, l * D:(l + 1) * D], w_in[:, l, :], ident[:, :])
            for c in range(3):
                nc.tensor.transpose(pA[:, c * D:(c + 1) * D], wih_in[:, c, :], ident[:, :])
            for c in range(3):
                last = nc.tensor.transpose(pR[:, c * D:(c + 1) * D], whh_in[:, c, :], ident[:, :])
            last.then_inc(s_wt, 1)
            pe.wait_ge(s_wtc, 3)
            for l, bank in enumerate((pZ, pHN, pIN, pH)):
                nc.tensor.matmul(bank[:, 0:3 * D], wT[:, l, :], wihT[:, :], start=True, stop=True).then_inc(s_wf, 1)
            pe.wait_ge(s_v, V_SLOTS)
            for j in range(TILES):
                nc.tensor.transpose(pA[:, j * NB:(j + 1) * NB], slot_dl[0:NB, j * P:(j + 1) * P], ident[0:NB, 0:NB])
            for j in range(TILES):
                last = nc.tensor.transpose(pA[:, (TILES + j) * NB:(TILES + j + 1) * NB],
                                           slot_src[0:NB, j * P:(j + 1) * P], ident[0:NB, 0:NB])
            last.then_inc(s_tab, 1)
            pe.wait_ge(s_v, V_CHECKS)
            pe.wait_ge(s_wfc, L)
            nc.tensor.matmul(pR[0:1, 0:1], checks[0:NB, :], ones[0:NB, 0:1], start=True, stop=True).then_inc(s_flag, 1)

            def at_least(s, value, start):
                if not start:
                    pe.wait_ge(s, value)

            def turn_h(l, b, u, loads, start):
                g = l * NB + b
                pe.wait_ge(s_load[u], 16 * loads)
                at_least(s_hhi, g, start)
                for k in range(RPP):
                    last = nc.tensor.transpose(pH[:, k * ROWS:(k + 1) * ROWS], h_rows[:, u, k * D:(k + 1) * D],
                                               ident[0:ROWS, 0:ROWS])
                last.then_inc(s_pH, 1)

            def sum_edges(l, b, u, start):
                g = l * NB + b
                pe.wait_ge(s_glo, g + 1)
                pe.wait_ge(s_sel, g + 1)
                at_least(s_agg, g, start)
                passes = [(part, j) for j in range(TILES) for part in (g_hi, g_lo)]
                for k, (part, j) in enumerate(passes):
                    last = nc.tensor.matmul(pA[:, 0:BLK], part[:, u, j, :], sel[:, u, j, :],
                                            start=k == 0, stop=k == len(passes) - 1)
                last.then_inc(s_pA, 1)

            def gates(l, b, u, start):
                g = l * NB + b
                pe.wait_ge(s_hlo, g + 1)
                pe.wait_ge(s_alo, g + 1)

                def product(bank, c, sides):
                    passes = []
                    for side in sides:
                        x_hi, x_lo, w_hi, w_lo = {
                            "in": (a_hi, a_lo, wf_hi[:, l, c * D:(c + 1) * D], wf_lo[:, l, c * D:(c + 1) * D]),
                            "state": (h_hi, h_lo, whh_hi[:, c * D:(c + 1) * D], whh_lo[:, c * D:(c + 1) * D])}[side]
                        passes += [(w_hi, x_hi), (w_hi, x_lo), (w_lo, x_hi)]
                    for k, (w, xx) in enumerate(passes):
                        last = nc.tensor.matmul(bank[:, 0:BLK], w, xx[:, u, :], start=k == 0, stop=k == len(passes) - 1)
                    return last

                at_least(s_r, g, start)
                product(pR, 0, ("in", "state")).then_inc(s_R, 1)
                at_least(s_t1, g, start)
                product(pHN, 2, ("state",)).then_inc(s_HN, 1)
                at_least(s_t2, g, start)
                product(pIN, 2, ("in",)).then_inc(s_IN, 1)
                at_least(s_z, g, start)
                product(pZ, 1, ("in", "state")).then_inc(s_Z, 1)

            def turn_back(l, b, u, start):
                g = l * NB + b
                pe.wait_ge(s_new, g + 1)
                if l == L - 1:
                    if start:
                        pe.wait_ge(s_o, l * NB)
                    else:
                        pe.wait_ge(s_y, b)
                else:
                    at_least(s_o, g, start and l == 0)
                for k in range(RPP):
                    last = nc.tensor.transpose(pO[0:ROWS, k * D:(k + 1) * D], newT[:, u, k * ROWS:(k + 1) * ROWS],
                                               ident[:, :])
                last.then_inc(s_pO, 1)

            def fast_path():
                for l in range(L):
                    def step(i, u, first, last):
                        start = first and l == 0
                        if first:
                            turn_h(l, 0, 0, GROUPS * l + 1, start)
                            turn_h(l, 1, 1, GROUPS * l + 1, False)
                            sum_edges(l, 0, 0, start)
                        if exists(i, u, 2):
                            nb, nu, ni = after(i, u, 2)
                            turn_h(l, nb, nu, GROUPS * l + ni + 1, False)
                        if not last:
                            sum_edges(l, *after(i, u)[:2], False)
                        gates(l, RING * i + u, u, start)
                        if not first:
                            pb, pu, _ = after(i, u, -1)
                            turn_back(l, pb, pu, isinstance(i, int) and pb == 0)
                        if last:
                            turn_back(l, RING * i + u, u, False)

                    blocks(pe, step)

            def general_path():
                for l in range(L):
                    def edge_row(r, first):
                        k = l * NCH + r
                        pe.wait_ge(s_ediag, k + 1)
                        nc.tensor.matmul(pZ[0:CHUNK, 0:CHUNK], ones[0:CHUNK, 0:CHUNK], e_diag[:, :],
                                         start=True, stop=True).then_inc(s_ebc, 1)
                        pe.wait_ge(s_ev, 5 * k + 2)
                        pe.wait_ge(s_ego[l], 2 * 16 * (r + 1))
                        nc.tensor.matmul(pHN[0:CHUNK, 0:D], e_same[:, :], e_rows[:, :],
                                         start=True, stop=True).then_inc(s_esum, 1)

                    edge_row(0, True)
                    with pe.Fori(1, NCH) as r:
                        edge_row(r, False)

                    def one(b, first):
                        start = first and l == 0
                        turn_h(l, b, 0, l * NB + b + 1, start)
                        pe.wait_ge(s_agld, 16 * (l * NB + b + 1))
                        at_least(s_agg, l * NB + b, start)
                        for k in range(RPP):
                            last = nc.tensor.transpose(pA[:, k * ROWS:(k + 1) * ROWS], y_rows[:, 1, k * D:(k + 1) * D],
                                                       ident[0:ROWS, 0:ROWS])
                        last.then_inc(s_pA, 1)
                        gates(l, b, 0, start)
                        turn_back(l, b, 0, first)

                    one_by_one(pe, one)

            pe.wait_ge(s_v, V_FLAG)
            flag = pe.value_load(flag_i[0:1, 0:1])
            with pe.If(flag == 0):
                fast_path()
            with pe.Else():
                general_path()

        @block.scalar
        def _(act):
            act.wait_ge(s_wt, 1)
            nc.scalar.copy(wT[:, :, :].rearrange("p l d -> p (l d)"), pH[:, 0:L * D]).then_inc(s_wtc, 1)
            nc.scalar.copy(wihT[:, :], pA[:, 0:3 * D]).then_inc(s_wtc, 1)
            nc.scalar.copy(whh_hi[:, :], pR[:, 0:3 * D]).then_inc(s_wtc, 1)
            for l, bank in enumerate((pZ, pHN, pIN, pH)):
                act.wait_ge(s_wf, l + 1)
                nc.scalar.copy(wf_hi[:, l, :], bank[:, 0:3 * D]).then_inc(s_wfc, 1)

            def copy_h(l, b, u):
                act.wait_ge(s_pH, l * NB + b + 1)
                nc.scalar.copy(hT[:, u, :], pH[:, 0:BLK]).then_inc(s_hT, 1)
                nc.scalar.copy(h_hi[:, u, :], pH[:, 0:BLK]).then_inc(s_hhi, 1)

            def high_gathered(l, b, u, gathers):
                act.wait_ge(s_gath[u], 16 * TILES * gathers)
                nc.scalar.copy(g_hi[:, u, :, :].rearrange("p j d -> p (j d)"),
                               gath[:, u, :, :].rearrange("p j d -> p (j d)")).then_inc(s_ghi, 1)

            def high_part(l, b, u):
                act.wait_ge(s_agg, l * NB + b + 1)
                nc.scalar.copy(a_hi[:, u, :], aggT[:, u, :]).then_inc(s_ahi, 1)

            def r_gate(l, b, u):
                act.wait_ge(s_R, l * NB + b + 1)
                nc.scalar.activation(rg[:, :], pR[:, 0:BLK], ACT.Sigmoid, bias=bsum[:, 0:1]).then_inc(s_r, 1)

            def n_and_z(l, b, u):
                g = l * NB + b
                act.wait_ge(s_t2, g + 1)
                nc.scalar.activation(ng[:, :], t2[:, :], ACT.Tanh, bias=bih[:, 2:3]).then_inc(s_n, 1)
                act.wait_ge(s_Z, g + 1)
                nc.scalar.activation(zg[:, :], pZ[:, 0:BLK], ACT.Sigmoid, bias=bsum[:, 1:2]).then_inc(s_z, 1)

            def rows_out(l, b, u, stored):
                g = l * NB + b
                if stored is not None:
                    act.wait_ge(s_store[u], 16 * stored)
                if l < L - 1:
                    act.wait_ge(s_pO, g + 1)
                    nc.scalar.copy(o_rows[:, u, :], pO[0:ROWS, 0:RPP * D]).then_inc(s_o, 1)
                else:
                    act.wait_ge(s_nmr, b + 1)
                    for k in range(RPP):
                        last = nc.scalar.activation(o_rows[:, u, k * D:(k + 1) * D], y_rows[:, u, k * D:(k + 1) * D],
                                                    ACT.Identity, bias=nmr[:, u, k:k + 1], scale=rstd[:, u, k:k + 1])
                    last.then_inc(s_o, 1)

            def fast_path():
                for l in range(L):
                    lag = NLAG + 1 if l == L - 1 else 1

                    def earlier(i):
                        return None if l == 0 and isinstance(i, int) and i == 0 else GROUPS * l + i

                    def step(i, u, first, last):
                        if first:
                            copy_h(l, 0, 0)
                            copy_h(l, 1, 1)
                            high_gathered(l, 0, 0, GROUPS * l + 1)
                            high_part(l, 0, 0)
                            high_gathered(l, 1, 1, GROUPS * l + 1)
                            high_gathered(l, 2, 2, GROUPS * l + 1)
                        r_gate(l, RING * i + u, u)
                        if exists(i, u, 2):
                            copy_h(l, *after(i, u, 2)[:2])
                        if not last:
                            high_part(l, *after(i, u)[:2])
                        if exists(i, u, 3):
                            nb, nu, ni = after(i, u, 3)
                            high_gathered(l, nb, nu, GROUPS * l + ni + 1)
                        n_and_z(l, RING * i + u, u)
                        if exists_before(i, u, lag):
                            pb, pu, pi = after(i, u, -lag)
                            rows_out(l, pb, pu, earlier(pi))

                    blocks(act, step)
                    for k in range(lag, 0, -1):
                        pb, pu, pi = after(GROUPS, 0, -k)
                        rows_out(l, pb, pu, earlier(pi))

            def general_path():
                for l in range(L):
                    def one(b, first):
                        copy_h(l, b, 0)
                        high_part(l, b, 0)
                        r_gate(l, b, 0)
                        n_and_z(l, b, 0)
                        rows_out(l, b, 0, None if first and l == 0 else l * NB + b)

                    one_by_one(act, one)

            act.wait_ge(s_v, V_FLAG)
            flag = act.value_load(flag_i[0:1, 0:1])
            with act.If(flag == 0):
                fast_path()
            with act.Else():
                general_path()

        @block.vector
        def _(dve):
            steps = [0]

            def done(ins):
                steps[0] += 1
                ins.then_inc(s_v, 1)
                dve.wait_ge(s_v, steps[0])

            v = nc.vector
            n_ = slice(0, NB)
            dve.wait_ge(s_edges, 4 * 16)
            dve.wait_ge(s_const, 5)
            firsts = dst_i[0:EP, :].rearrange("p (m j) -> p m j", j=CHUNK)[:, :, 0]
            done(v.tensor_copy(stat[0:EP, 0:CPR], firsts))
            for m in range(CPR):
                last = v.tensor_scalar(diag[0:EP, m, 0:EP], ident[0:EP, 0:EP], stat[0:EP, m:m + 1], None, ALU.mult)
            done(last)
            assert steps[0] == V_DIAG
            done(v.tensor_tensor(tmp_a[0:EP, 0:EC], nxt_i[0:EP, :], dst_i[0:EP, :], ALU.subtract))
            done(v.tensor_tensor(tmp_b[0:EP, 0:EC], src_i[0:EP, :], dst_i[0:EP, :], ALU.not_equal))
            done(v.scalar_tensor_tensor(tmp_c[0:EP, 0:EC], tmp_a[0:EP, 0:EC], 1.0, tmp_b[0:EP, 0:EC],
                                        ALU.is_equal, ALU.mult, accum_out=sums[0:EP, 0:1]))
            done(v.tensor_scalar(tmp_c[0:EP, 0:EC], tmp_a[0:EP, 0:EC], 0.0, None, ALU.is_equal, ALU.add,
                                 accum_out=sums[0:EP, 1:2]))
            done(v.tensor_scalar(tmp_c[0:EP, 0:EC], tmp_a[0:EP, 0:EC], 1.0, None, ALU.is_equal, ALU.add,
                                 accum_out=sums[0:EP, 2:3]))
            dve.wait_ge(s_bc, 1)
            bc = pO[n_, 0:CPR * P].rearrange("p (m q) -> p m q", q=P)[:, :, 0:EP]
            done(v.tensor_scalar(tmp_c[n_, 0:CPR * EP].rearrange("p (m q) -> p m q", q=EP), bc, blk_start[n_, :], None,
                                 ALU.is_lt, ALU.add, accum_out=stat[n_, 5:6]))
            done(v.tensor_scalar(stat[n_, 6:7], stat[n_, 5:6], -1.0, 0.0, ALU.add, ALU.max))
            for m in range(WCH):
                last = v.tensor_scalar(chunk_i[n_, m:m + 1], stat[n_, 6:7], float(m), None, ALU.add)
            done(last)
            assert steps[0] == V_ROWS
            dve.wait_ge(s_win, WCH * 16)
            done(v.tensor_copy(winf[n_, :], win_dst[n_, :]))
            done(v.tensor_tensor(tmp_b[n_, :], winf[n_, 0:WIN], winf[n_, 1:WIN + 1], ALU.is_equal))
            done(v.tensor_scalar(tmp_a[n_, :], winf[n_, 0:WIN], blk_start[n_, :], None, ALU.subtract))
            done(v.scalar_tensor_tensor(tmp_c[n_, :], tmp_a[n_, :], 0.0, tmp_b[n_, :], ALU.is_ge, ALU.mult))
            done(v.scalar_tensor_tensor(tmp_b[n_, :], tmp_a[n_, :], float(BLK), tmp_c[n_, :], ALU.is_lt, ALU.mult,
                                        accum_out=sums[n_, 3:4]))
            done(v.tensor_scalar(dl_i[n_, :], tmp_a[n_, :], 0.0, float(BLK - 1), ALU.max, ALU.min))
            done(v.tensor_scalar(key_i[n_, :], dl_i[n_, :], 16, 1 << 30, ALU.logical_shift_left, ALU.bitwise_or))
            dve.wait_ge(s_w, 5 * 16)
            done(v.tensor_tensor(bsum[:, :], bih[:, :], bhh[:, :], ALU.add))
            assert steps[0] == V_BIAS
            dve.wait_ge(s_wtc, 3)
            v.tensor_tensor(whh_lo[:, :], pR[:, 0:3 * D], whh_hi[:, :].bitcast(F32), ALU.subtract)
            dve.wait_ge(s_wfc, L)
            for l, bank in enumerate((pZ, pHN, pIN, pH)):
                last = v.tensor_tensor(wf_lo[:, l, :], bank[:, 0:3 * D], wf_hi[:, l, :].bitcast(F32), ALU.subtract)
            done(last)
            assert steps[0] == V_WEIGHTS
            dve.wait_ge(s_winsrc, WCH * 16)
            done(v.tensor_tensor(dl_i[n_, :], key_i[n_, :], win_src[n_, :], ALU.bitwise_or))
            done(v.tensor_tensor(tmp_a[n_, :], dl_i[n_, :].bitcast(F32), tmp_b[n_, :], ALU.mult))
            cur, nxt = tmp_a, tmp_c
            width = LIVE
            for r in range(CAP // 8):
                done(v.max(keys[n_, 8 * r:8 * r + 8], cur[n_, 0:width]))
                if r < CAP // 8 - 1:
                    width -= SHRINK
                    done(v.match_replace(nxt[n_, 0:width], keys[n_, 8 * r:8 * r + 8], cur[n_, 0:width], 0.0))
                    cur, nxt = nxt, cur
            done(v.tensor_scalar(tmp_b[n_, 0:CAP], keys[n_, :], 0.0, None, ALU.is_gt, ALU.add, accum_out=sums[n_, 4:5]))
            ki = keys[n_, :].bitcast(I32)
            v.tensor_scalar(slot_dl_i[n_, :], ki, 16, None, ALU.logical_shift_right)
            v.tensor_scalar(slot_ok_i[n_, :], ki, 30, None, ALU.logical_shift_right)
            done(v.tensor_scalar(slot_src_i[n_, :], ki, 0xFFFF, None, ALU.bitwise_and))
            v.tensor_scalar(slot_dl[n_, :], slot_dl_i[n_, :], -16384.0, None, ALU.add)
            done(v.tensor_scalar(tmp_b[n_, 0:CAP], slot_ok_i[n_, :], -65536.0, 65536.0, ALU.mult, ALU.add))
            done(v.tensor_tensor(slot_src[n_, :], tmp_b[n_, 0:CAP], slot_src_i[n_, :], ALU.add))
            assert steps[0] == V_SLOTS
            dve.wait_ge(s_tab, 1)
            v.tensor_copy(edge_dl[:, :, :].rearrange("p j b -> p (j b)"), pA[:, 0:TILES * NB])
            done(v.tensor_copy(edge_src[:, :, :].rearrange("p j b -> p (j b)"), pA[:, TILES * NB:2 * TILES * NB]))
            assert steps[0] == V_TABLES
            done(v.tensor_tensor(checks[n_, :], sums[n_, 0:1], sums[n_, 1:2], ALU.subtract))
            done(v.scalar_tensor_tensor(checks[n_, :], checks[n_, :], float(EC), sums[n_, 2:3], ALU.add, ALU.subtract))
            done(v.scalar_tensor_tensor(checks[n_, :], sums[n_, 3:4], sums[n_, 4:5], checks[n_, :],
                                        ALU.not_equal, ALU.add))
            assert steps[0] == V_CHECKS
            dve.wait_ge(s_flag, 1)
            done(v.tensor_tensor(flag_i[0:1, 0:1], pR[0:1, 0:1], dst_i[0:1, 0:1], ALU.add))
            assert steps[0] == V_FLAG

            def select(b, u, j):
                ins = v.tensor_scalar(sel[:, u, j, :], node_of_col[:, :], edge_dl[:, j, bass.ds(b, 1)], None, ALU.is_equal)
                if j == TILES - 1:
                    ins.then_inc(s_sel, 1)

            def low_part(l, b, u):
                dve.wait_ge(s_ahi, l * NB + b + 1)
                v.tensor_tensor(a_lo[:, u, :], aggT[:, u, :], a_hi[:, u, :].bitcast(F32), ALU.subtract).then_inc(s_alo, 1)

            def aggregate(l, b, u):
                g = l * NB + b
                dve.wait_ge(s_hT, g + 1)
                dve.wait_ge(s_pA, g + 1)
                v.tensor_tensor(aggT[:, u, :], pA[:, 0:BLK], hT[:, u, :], ALU.add).then_inc(s_agg, 1)

            def n_argument(l, b, u, start, between=lambda: None):
                g = l * NB + b
                if not start:
                    dve.wait_ge(s_new, g)
                dve.wait_ge(s_HN, g + 1)
                dve.wait_ge(s_r, g + 1)
                v.scalar_tensor_tensor(t1[:, :], pHN[:, 0:BLK], bhh[:, 2:3], rg[:, :],
                                       ALU.add, ALU.mult).then_inc(s_t1, 1)
                between()
                dve.wait_ge(s_IN, g + 1)
                dve.wait_ge(s_t1, g + 1)
                v.tensor_tensor(t2[:, :], pIN[:, 0:BLK], t1[:, :], ALU.add).then_inc(s_t2, 1)

            def mix(l, b, u, fill_d=lambda: None, fill_e=lambda: None):
                g = l * NB + b
                dve.wait_ge(s_n, g + 1)
                v.tensor_tensor(t1[:, :], hT[:, u, :], ng[:, :], ALU.subtract).then_inc(s_d, 1)
                fill_d()
                dve.wait_ge(s_z, g + 1)
                dve.wait_ge(s_d, g + 1)
                v.tensor_tensor(t2[:, :], zg[:, :], t1[:, :], ALU.mult).then_inc(s_e, 1)
                fill_e()
                dve.wait_ge(s_e, g + 1)
                v.tensor_tensor(newT[:, u, :], t2[:, :], ng[:, :], ALU.add).then_inc(s_new, 1)

            def residual(l, b, u, loads):
                dve.wait_ge(s_pO, l * NB + b + 1)
                dve.wait_ge(s_xld[u], 16 * loads)
                v.scalar_tensor_tensor(y_rows[:, u, :], x_rows[:, u, :], 2.0, pO[0:ROWS, 0:RPP * D],
                                       ALU.mult, ALU.add).then_inc(s_y, 1)

            def row_stats(b, u):
                dve.wait_ge(s_y, b + 1)
                for k in range(RPP):
                    last = v.bn_stats(bn[:, u, k, :], y_rows[:, u, k * D:(k + 1) * D])
                last.then_inc(s_bn, 1)

            def moments(b, u):
                dve.wait_ge(s_bn, b + 1)
                v.tensor_tensor(mv[:, u, :, 0], bn[:, u, :, 1], bn[:, u, :, 4], ALU.add)
                v.scalar_tensor_tensor(mv[:, u, :, 1], bn[:, u, :, 2], D * EPS, bn[:, u, :, 5], ALU.add, ALU.add)
                v.tensor_tensor(mv[:, u, :, 2], bn[:, u, :, 1], bn[:, u, :, 4], ALU.subtract).then_inc(s_mv, 1)

            def squared_difference(b, u):
                dve.wait_ge(s_mv, 2 * b + 1)
                v.scalar_tensor_tensor(mv[:, u, :, 3], mv[:, u, :, 2], 0.25, mv[:, u, :, 2],
                                       ALU.mult, ALU.mult).then_inc(s_mv, 1)

            def variance(b, u):
                dve.wait_ge(s_mv, 2 * b + 2)
                v.scalar_tensor_tensor(veps[:, u, :], mv[:, u, :, 1], 1.0 / D, mv[:, u, :, 3],
                                       ALU.mult, ALU.add).then_inc(s_eps, 1)

            def shift(b, u):
                dve.wait_ge(s_rstd, b + 1)
                v.scalar_tensor_tensor(nmr[:, u, :], mv[:, u, :, 0], -0.5, rstd[:, u, :],
                                       ALU.mult, ALU.mult).then_inc(s_nmr, 1)

            def fast_path():
                for l in range(L):
                    def step(i, u, first, last):
                        if first:
                            for early in range(3):
                                for j in range(TILES):
                                    select(early, early, j)
                            aggregate(l, 0, 0)
                            low_part(l, 0, 0)

                        def select_later(j):
                            if exists(i, u, 3):
                                select(*after(i, u, 3)[:2], j)

                        def on_rows(work):
                            if l == L - 1 and exists_before(i, u, NLAG):
                                work(*after(i, u, -NLAG)[:2])

                        rows_too = l == L - 1 and exists_before(i, u, NLAG - 1)
                        if rows_too:
                            pb, pu, pi = after(i, u, 1 - NLAG)
                            residual(l, pb, pu, pi + 1)
                        on_rows(moments)

                        def beside_difference():
                            select_later(0)
                            on_rows(squared_difference)

                        def beside_product():
                            if not last:
                                aggregate(l, *after(i, u)[:2])
                            on_rows(variance)

                        if first:
                            beside_difference()
                            beside_product()
                        else:
                            mix(l, *after(i, u, -1)[:2], beside_difference, beside_product)
                        n_argument(l, RING * i + u, u, first and l == 0, lambda: select_later(1))
                        if not last:
                            low_part(l, *after(i, u)[:2])
                        if l == L - 1 and exists_before(i, u, NLAG + 1):
                            shift(*after(i, u, -NLAG - 1)[:2])
                        if rows_too:
                            row_stats(pb, pu)
                        if last:
                            mix(l, RING * i + u, u)

                    blocks(dve, step)
                    if l == L - 1:
                        for k in range(NLAG + 1, 0, -1):
                            pb, pu, pi = after(GROUPS, 0, -k)
                            if k < NLAG:
                                residual(l, pb, pu, pi + 1)
                                row_stats(pb, pu)
                            if k <= NLAG:
                                for work in (moments, squared_difference, variance):
                                    work(pb, pu)
                            shift(pb, pu)

            def general_path():
                dve.wait_ge(s_zero, 8)
                for l in range(L):
                    def edge_row(r, first):
                        k = l * NCH + r
                        dve.wait_ge(s_eld[l], 2 * 16 * (r + 1))
                        v.tensor_copy(e_dstf[:, :], e_dst[:, :]).then_inc(s_ev, 1)
                        dve.wait_ge(s_ev, 5 * k + 1)
                        v.tensor_scalar(e_diag[:, :], ident[0:CHUNK, 0:CHUNK], e_dstf[:, :], None,
                                        ALU.mult).then_inc(s_ediag, 1)
                        dve.wait_ge(s_ebc, k + 1)
                        v.tensor_scalar(e_same[:, :], pZ[0:CHUNK, 0:CHUNK], e_dstf[:, :], None,
                                        ALU.is_equal).then_inc(s_ev, 1)
                        dve.wait_ge(s_ev, 5 * k + 2)
                        v.scalar_tensor_tensor(e_junk[:, :], e_same[:, :], 1.0, before[:, :], ALU.mult, ALU.mult,
                                               accum_out=e_dup[:, :]).then_inc(s_ev, 1)
                        dve.wait_ge(s_ev, 5 * k + 3)
                        v.scalar_tensor_tensor(e_at[:, :], e_dup[:, :], 65536.0, e_dstf[:, :],
                                               ALU.mult, ALU.add).then_inc(s_ev, 1)
                        dve.wait_ge(s_esum, k + 1)
                        v.tensor_tensor(e_new[:, :], pHN[0:CHUNK, 0:D], e_old[:, :], ALU.add).then_inc(s_ev, 1)

                    edge_row(0, True)
                    with dve.Fori(1, NCH) as r:
                        edge_row(r, False)

                    def one(b, first):
                        dve.wait_ge(s_pA, l * NB + b + 1)
                        v.tensor_copy(aggT[:, 0, :], pA[:, 0:BLK]).then_inc(s_agg, 1)
                        low_part(l, b, 0)
                        n_argument(l, b, 0, first and l == 0)
                        mix(l, b, 0)
                        if l == L - 1:
                            residual(l, b, 0, b + 1)
                            for work in (row_stats, moments, squared_difference, variance, shift):
                                work(b, 0)

                    one_by_one(dve, one)

            flag = dve.value_load(flag_i[0:1, 0:1])
            with dve.If(flag == 0):
                fast_path()
            with dve.Else():
                general_path()


_INS = ['x', 'src', 'dst', 'L0_gnn_weight', 'L0_gnn_w_ih', 'L0_gnn_w_hh', 'L0_gnn_b_ih', 'L0_gnn_b_hh']
_OUTS = [((50000, 128), 'float32')]


def kernel(**inputs):
    import numpy as _np
    import concourse.bacc as _bacc
    from concourse import mybir as _mybir
    from concourse.bass_utils import run_bass_kernel_spmd as _run

    nc = _bacc.Bacc("TRN2", target_bir_lowering=False, num_devices=1)
    arrays, args = {}, []
    for name in _INS:
        a = _np.ascontiguousarray(inputs[name])
        arrays[f"in_{name}_dram"] = a
        args.append(nc.dram_tensor(f"in_{name}_dram", a.shape, _mybir.dt.from_np(a.dtype), kind="ExternalInput").ap())
    for i, (shape, dtype) in enumerate(_OUTS):
        dt = _mybir.dt.from_np(_np.dtype(dtype))
        args.append(nc.dram_tensor(f"out_{i}_dram", shape, dt, kind="ExternalOutput").ap())
    build(nc, *args)
    r = _run(nc, [arrays], core_ids=[0])
    got = tuple(r.results[0][f"out_{i}_dram"] for i in range(len(_OUTS)))
    return got[0]
```

```python
from contextlib import ExitStack

import concourse.bass as bass
from concourse import mybir

F32 = mybir.dt.float32
F32R = mybir.dt.float32r
I32 = mybir.dt.int32
ALU = mybir.AluOpType
ACT = mybir.ActivationFunctionType

P = 128
BANK = 512
D = 128
ROWS = 100
RPP = 4
BLK = ROWS * RPP
TILES = 2
ENDS = (ROWS, 64)
CAP = TILES * P
RING = 5
CHUNK = 120
WCH = 7
WIN = CHUNK * WCH
LIVE = CHUNK + BLK + CAP
SHRINK = 16
EPS = 1e-5
NLAG = 3

V_DIAG = 2
V_ROWS = 10
V_BIAS = V_ROWS + 8
V_WEIGHTS = V_BIAS + 1
V_SLOTS = V_WEIGHTS + 2 + 2 * (CAP // 8) - 1 + 4
V_TABLES = V_SLOTS + 1
V_CHECKS = V_TABLES + 2 + TILES
V_FLAG = V_CHECKS + 1


def build(nc, x, src, dst, weight, w_ih, w_hh, b_ih, b_hh, out):
    N = x.shape[0]
    E = src.shape[0]
    L = weight.shape[0]
    NB = N // BLK
    GROUPS = NB // RING
    EP = NB
    EC = E // EP
    CPR = EC // CHUNK
    NCH = E // CHUNK
    assert NB * BLK == N and GROUPS * RING == NB and EP * EC == E and CPR * CHUNK == EC and NB <= P

    edge_sum = nc.dram_tensor("edge_sum", [N, D], F32, kind="Internal").ap()
    states = [x] + [nc.dram_tensor(f"state_{l}", [N, D], F32, kind="Internal").ap() for l in range(1, L)]

    def rows_of(t, b):
        v = t.rearrange("(b p k) f -> b p (k f)", p=ROWS, k=RPP)
        return v[bass.ds(b, 1), :, :].rearrange("b p m -> (b p) m")

    ctx = ExitStack()
    with ctx:
        def sb(name, shape, dt=F32):
            return ctx.enter_context(nc.sbuf_tensor(name, shape, dt))

        def ps(name, cols):
            return ctx.enter_context(nc.psum_tensor(name, [P, cols], F32))

        def sem(name):
            return ctx.enter_context(nc.semaphore(name))

        ident = sb("ident", [P, P])
        ident_r = sb("ident_r", [P, P], F32R)
        ones = sb("ones", [P, P])
        node_of_col = sb("node_of_col", [P, BLK])
        blk_start = sb("blk_start", [P, 1])
        w_in = sb("w_in", [P, L, D])
        wT = sb("wT", [P, L, D])
        wih_in = sb("wih_in", [P, 3, D])
        whh_in = sb("whh_in", [P, 3, D])
        wihT = sb("wihT", [P, 3 * D])
        whh_hi = sb("whh_hi", [P, 3 * D], F32R)
        whh_lo = sb("whh_lo", [P, 3 * D], F32R)
        wf_hi = sb("wf_hi", [P, L, 3 * D], F32R)
        wf_lo = sb("wf_lo", [P, L, 3 * D], F32R)
        bih = sb("bih", [P, 3])
        bhh = sb("bhh", [P, 3])
        bsum = sb("bsum", [P, 3])
        dst_i = sb("dst_i", [P, EC], I32)
        nxt_i = sb("nxt_i", [P, EC], I32)
        src_i = sb("src_i", [P, EC], I32)
        win_dst = sb("win_dst", [P, WIN + 1], I32)
        win_src = sb("win_src", [P, WIN], I32)
        winf = sb("winf", [P, WIN + 1])
        dl_i = sb("dl_i", [P, WIN], I32)
        diag = sb("diag", [P, CPR, P])
        stat = sb("stat", [P, 8])
        sums = sb("sums", [P, 8])
        chunk_i = sb("chunk_i", [P, WCH], I32)
        keys = sb("keys", [P, CAP])
        slot_dl_i = sb("slot_dl_i", [P, CAP], I32)
        slot_src_i = sb("slot_src_i", [P, CAP], I32)
        slot_ok_i = sb("slot_ok_i", [P, CAP], I32)
        slot_dl = sb("slot_dl", [P, CAP])
        slot_src = sb("slot_src", [P, CAP])
        edge_dl = sb("edge_dl", [P, TILES, NB])
        edge_src = sb("edge_src", [P, TILES, NB], I32)
        idx = sb("idx", [P, TILES, RING], I32)
        checks = sb("checks", [P, 1])
        flag_i = sb("flag_i", [1, 1], I32)
        before = sb("before", [CHUNK, CHUNK])
        e_src = sb("e_src", [CHUNK, 1], I32)
        e_dst = sb("e_dst", [CHUNK, 1], I32)
        e_dstf = sb("e_dstf", [CHUNK, 1])
        e_diag = sb("e_diag", [CHUNK, CHUNK])
        e_same = sb("e_same", [CHUNK, CHUNK])
        e_junk = sb("e_junk", [CHUNK, CHUNK])
        e_dup = sb("e_dup", [CHUNK, 1])
        e_at = sb("e_at", [CHUNK, 1], I32)
        e_rows = sb("e_rows", [CHUNK, D])
        e_old = sb("e_old", [CHUNK, D])
        e_new = sb("e_new", [CHUNK, D])
        zeros = sb("zeros", [ROWS, RPP * D])
        h_rows = sb("h_rows", [ROWS, RING, RPP * D])
        gath = sb("gath", [P, RING, TILES, D])
        g_hi = sb("g_hi", [P, RING, TILES, D], F32R)
        g_lo = sb("g_lo", [P, RING, TILES, D], F32R)
        sel = sb("sel", [P, RING, TILES, BLK], F32R)
        hT = sb("hT", [P, RING, BLK])
        h_hi = sb("h_hi", [P, RING, BLK], F32R)
        h_lo = sb("h_lo", [P, RING, BLK], F32R)
        aggT = sb("aggT", [P, RING, BLK])
        a_hi = sb("a_hi", [P, RING, BLK], F32R)
        a_lo = sb("a_lo", [P, RING, BLK], F32R)
        rg = sb("rg", [P, BLK])
        zg = sb("zg", [P, BLK])
        ng = sb("ng", [P, BLK])
        t1 = sb("t1", [P, BLK])
        t2 = sb("t2", [P, BLK])
        newT = sb("newT", [P, RING, BLK])
        new_flat = newT[:, :, :].rearrange("p r n -> p (r n)")
        h_flat = hT[:, :, :].rearrange("p r n -> p (r n)")
        tmp_a, tmp_b = new_flat[:, 0:WIN], new_flat[:, WIN:2 * WIN]
        tmp_c, key_i = h_flat[:, 0:WIN], h_flat[:, WIN:2 * WIN].bitcast(I32)
        o_rows = sb("o_rows", [ROWS, RING, RPP * D])
        x_rows = sb("x_rows", [ROWS, RING, RPP * D])
        y_rows = sb("y_rows", [ROWS, RING, RPP * D])
        bn = sb("bn", [ROWS, RING, RPP, 6])
        mv = sb("mv", [ROWS, RING, RPP, 4])
        veps = sb("veps", [ROWS, RING, RPP])
        rstd = sb("rstd", [ROWS, RING, RPP])
        nmr = sb("nmr", [ROWS, RING, RPP])
        mhalf = sb("mhalf", [ROWS, RPP])

        pH = ps("pH", BANK)
        pA = ps("pA", 2 * BANK)
        pR = ps("pR", BANK)
        pZ = ps("pZ", BANK)
        pHN = ps("pHN", BANK)
        pIN = ps("pIN", BANK)
        pO = ps("pO", BANK)

        def edge_bank(u):
            return pA[:, (u % 2) * BANK:(u % 2) * BANK + BLK]

        def of_rows(columns, j):
            return columns.rearrange("p (k r) -> p k r", k=RPP)[:, :, 0:ENDS[j]]

        def selection(u, j):
            return sel[:, u, j, 0:RPP * ENDS[j]].rearrange("p (k r) -> p k r", k=RPP)

        s_w = sem("weights_loaded")
        s_edges = sem("edges_loaded")
        s_const = sem("constants_made")
        s_identr = sem("identity_rounded")
        s_wt = sem("weight_transposes_done")
        s_wtc = sem("weight_transposes_copied")
        s_wf = sem("fused_weights_done")
        s_wfc = sem("fused_weights_copied")
        s_v = sem("vector_setup_steps")
        s_bc = sem("row_firsts_broadcast")
        s_win = sem("dst_windows_gathered")
        s_winsrc = sem("src_windows_gathered")
        s_tab = sem("tables_transposed")
        s_load = [sem(f"rows_loaded_{u}") for u in range(RING)]
        s_xld = [sem(f"x_rows_loaded_{u}") for u in range(RING)]
        s_gath = [sem(f"edges_gathered_{u}") for u in range(RING)]
        s_store = [sem(f"rows_stored_{u}") for u in range(RING)]
        s_pH = sem("h_transposed")
        s_hT = sem("h_copied")
        s_hhi = sem("h_high_parts")
        s_hlo = sem("h_low_parts")
        s_ghi = sem("gathered_high_parts")
        s_glo = sem("gathered_low_parts")
        s_ahi = sem("agg_high_parts")
        s_alo = sem("agg_low_parts")
        s_sel = sem("selection_built")
        s_pA = sem("edges_summed")
        s_agg = sem("agg_made")
        s_R = sem("r_product")
        s_Z = sem("z_product")
        s_HN = sem("hn_product")
        s_IN = sem("in_product")
        s_r = sem("r_gate")
        s_z = sem("z_gate")
        s_n = sem("n_gate")
        s_t1 = sem("r_times_hn")
        s_t2 = sem("n_argument")
        s_d = sem("h_minus_n")
        s_e = sem("z_times_difference")
        s_new = sem("new_state")
        s_pO = sem("state_transposed_back")
        s_o = sem("rows_ready")
        s_y = sem("residual_added")
        s_bn = sem("row_stats")
        s_mv = sem("row_moments")
        s_eps = sem("variance_plus_eps")
        s_rstd = sem("rstd_made")
        s_nmr = sem("shift_made")
        s_zero = sem("gather_buffers_cleared")
        s_idx = sem("block_indices_copied")

        s_flag = sem("checks_added_up")
        s_sum0 = sem("edge_sum_cleared")
        s_eld = [sem(f"edge_rows_loaded_{l}") for l in range(L)]
        s_ego = [sem(f"edge_rows_gathered_{l}") for l in range(L)]
        s_ediag = sem("destinations_on_diagonal")
        s_ebc = sem("destinations_broadcast")
        s_esum = sem("edge_row_summed")
        s_ev = sem("edge_row_vector_steps")
        s_esc = sem("edge_row_scattered")
        s_agld = sem("edge_sums_loaded")

        block = ctx.enter_context(nc.Block())

        def blocks(eng, step):
            for u in range(RING):
                step(0, u, u == 0, False)
            with eng.Fori(1, GROUPS - 1) as i:
                for u in range(RING):
                    step(i, u, False, False)
            for u in range(RING):
                step(GROUPS - 1, u, False, u == RING - 1)

        def after(i, u, k=1):
            i, u = i + (u + k) // RING, (u + k) % RING
            return RING * i + u, u, i

        def exists(i, u, k):
            return not isinstance(i, int) or RING * i + u + k < NB

        def exists_before(i, u, k):
            return not isinstance(i, int) or RING * i + u >= k

        def one_by_one(eng, step):
            step(0, True)
            with eng.Fori(1, NB) as b:
                step(b, False)

        @block.sync
        def _(sp):
            sp.dma_start(dst_i[0:EP, :], dst.rearrange("(p j) -> p j", p=EP)).then_inc(s_edges, 16)
            sp.dma_start(src_i[0:EP, :], src.rearrange("(p j) -> p j", p=EP)).then_inc(s_edges, 16)
            sp.wait_ge(s_const, 1)
            sp.dma_start(nxt_i[0:EP - 1, :],
                         dst[1:1 + (EP - 1) * EC].rearrange("(p j) -> p j", j=EC)).then_inc(s_edges, 16)
            sp.dma_start(nxt_i[EP - 1:EP, 0:EC - 1],
                         dst[1 + (EP - 1) * EC:E].rearrange("(p j) -> p j", p=1)).then_inc(s_edges, 16)
            sp.dma_start(w_in[:, :, :], weight.rearrange("l i o -> i l o")).then_inc(s_w, 16)
            sp.dma_start(wih_in[:, :, :], w_ih.rearrange("(c o) k -> o c k", c=3)).then_inc(s_w, 16)
            sp.dma_start(whh_in[:, :, :], w_hh.rearrange("(c o) k -> o c k", c=3)).then_inc(s_w, 16)
            sp.dma_start(bih[:, :], b_ih.rearrange("(c o) -> o c", c=3), allow_slow_non_contiguous=True).then_inc(s_w, 16)
            sp.dma_start(bhh[:, :], b_hh.rearrange("(c o) -> o c", c=3), allow_slow_non_contiguous=True).then_inc(s_w, 16)

            def load(l, b, u):
                sp.dma_start(h_rows[:, u, :], rows_of(states[l], b)).then_inc(s_load[u], 16)

            def load_x(b, u):
                sp.dma_start(x_rows[:, u, :], rows_of(x, b)).then_inc(s_xld[u], 16)

            def store(l, b, u):
                sp.wait_ge(s_o, l * NB + b + 1)
                to = out if l == L - 1 else states[l + 1]
                sp.dma_start(rows_of(to, b), o_rows[:, u, :]).then_inc(s_store[u], 16)

            def fast_path():
                for l in range(L):
                    if l:
                        sp.wait_ge(s_pH, l * NB)
                    for u in range(RING):
                        if l:
                            sp.wait_ge(s_store[u], 16 * (GROUPS * (l - 1) + 1))
                        load(l, u, u)
                    if l:
                        for u in range(RING):
                            sp.wait_ge(s_store[u], 16 * GROUPS * l)
                    if l == L - 1:
                        for u in range(RING):
                            load_x(u, u)

                    def step(i, u, first, last):
                        if exists(i, u, RING):
                            sp.wait_ge(s_pH, l * NB + RING * i + u + 1)
                            sp.nop(nofuse=True)
                            load(l, RING * i + u + RING, u)
                        if l < L - 1:
                            if exists_before(i, u, 1):
                                store(l, *after(i, u, -1)[:2])
                            if isinstance(i, int) and RING * i + u == NB - 1:
                                store(l, NB - 1, RING - 1)
                        elif exists_before(i, u, NLAG + 1):
                            pb, pu, _ = after(i, u, -NLAG - 1)
                            store(l, pb, pu)
                            if exists(i, u, RING - NLAG - 1):
                                load_x(pb + RING, pu)

                    blocks(sp, step)
                    if l == L - 1:
                        for k in range(NLAG + 1, 0, -1):
                            pb, pu, _ = after(GROUPS, 0, -k)
                            store(l, pb, pu)
                for u in range(RING):
                    sp.wait_ge(s_store[u], 16 * GROUPS * L)

            def general_path():
                for l in range(L):
                    if l:
                        sp.wait_ge(s_store[0], 16 * NB * l)
                    with sp.Fori(0, NB) as b:
                        sp.dma_start(rows_of(edge_sum, b), zeros[:, :]).then_inc(s_sum0, 16)
                    sp.wait_ge(s_sum0, 16 * NB * (l + 1))

                    def edge_row(r, first):
                        if not (first and l == 0):
                            sp.wait_ge(s_esc, 16 * (l * NCH + r))
                            sp.nop(nofuse=True)
                        for arr, to in ((src, e_src), (dst, e_dst)):
                            rows = arr.rearrange("(r j o) -> r j o", j=CHUNK, o=1)
                            sp.dma_start(to[:, :], rows[bass.ds(r, 1), :, :].rearrange("r j o -> (r j) o")).then_inc(s_eld[l], 16)

                    edge_row(0, True)
                    with sp.Fori(1, NCH) as r:
                        edge_row(r, False)
                    sp.wait_ge(s_esc, 16 * NCH * (l + 1))

                    def one(b, first):
                        if not (first and l == 0):
                            sp.wait_ge(s_store[0], 16 * (l * NB + b))
                            sp.nop(nofuse=True)
                        load(l, b, 0)
                        if l == L - 1:
                            load_x(b, 0)
                        sp.dma_start(y_rows[:, 1, :], rows_of(edge_sum, b)).then_inc(s_agld, 16)
                        store(l, b, 0)

                    one_by_one(sp, one)
                sp.wait_ge(s_store[0], 16 * NB * L)

            sp.wait_ge(s_v, V_FLAG)
            flag = sp.value_load(flag_i[0:1, 0:1])
            with sp.If(flag == 0):
                fast_path()
            with sp.Else():
                general_path()

        @block.gpsimd
        def _(pool):
            nc.gpsimd.memset(nxt_i[:, :], N).then_inc(s_const, 1)
            nc.gpsimd.memset(ones[:, :], 1.0).then_inc(s_const, 1)
            nc.gpsimd.memset(ident[:, :], 0.0).then_inc(s_zero, 1)
            nc.gpsimd.iota(node_of_col[:, :], [[1, RPP], [RPP, ROWS]], base=0, channel_multiplier=0,
                           allow_small_or_imprecise_dtypes=True).then_inc(s_const, 1)
            nc.gpsimd.iota(blk_start[:, :], [[0, 1]], base=0, channel_multiplier=BLK,
                           allow_small_or_imprecise_dtypes=True).then_inc(s_const, 1)
            pool.wait_ge(s_zero, 1)
            nc.gpsimd.affine_select(out=ident[:, :], in_=ident[:, :], compare_op=ALU.not_equal, fill=1.0, base=0,
                                    pattern=[[-1, P]], channel_multiplier=1).then_inc(s_const, 1)
            nc.gpsimd.memset(win_dst[:, :], -1).then_inc(s_zero, 1)
            nc.gpsimd.memset(win_src[:, :], 0).then_inc(s_zero, 1)
            nc.gpsimd.memset(gath[:, :, :, :], 0.0).then_inc(s_zero, 1)
            nc.gpsimd.memset(mhalf[:, :], -0.5).then_inc(s_zero, 1)
            nc.gpsimd.memset(zeros[:, :], 0.0).then_inc(s_zero, 1)
            nc.gpsimd.memset(before[:, :], 1.0).then_inc(s_zero, 1)
            pool.wait_ge(s_zero, 7)
            nc.gpsimd.affine_select(out=before[:, :], in_=before[:, :], compare_op=ALU.is_gt, fill=0.0, base=0,
                                    pattern=[[-1, CHUNK]], channel_multiplier=1).then_inc(s_zero, 1)
            pool.wait_ge(s_v, V_ROWS)
            for arr, win, arrived in ((dst, win_dst, s_win), (src, win_src, s_winsrc)):
                for m in range(WCH):
                    pool.indirect_dma_start(
                        out=win[0:NB, m * CHUNK:(m + 1) * CHUNK], out_offset=None,
                        in_=arr.rearrange("(r j) -> r j", j=CHUNK),
                        in_offset=bass.IndirectOffsetOnAxis(ap=chunk_i[0:NB, m:m + 1], axis=0),
                        bounds_check=NCH - 1, oob_is_err=False).then_inc(arrived, 16)

            last_node = pool.to_reg(N - 1)

            def split_h(l, b, u):
                pool.wait_ge(s_hhi, l * NB + b + 1)
                nc.gpsimd.tensor_tensor(h_lo[:, u, :], hT[:, u, :], h_hi[:, u, :].bitcast(F32),
                                        ALU.subtract).then_inc(s_hlo, 1)

            def root(b, u):
                pool.wait_ge(s_eps, b + 1)
                nc.gpsimd.tensor_tensor(rstd[:, u, :], veps[:, u, :], mhalf[:, :], ALU.pow).then_inc(s_rstd, 1)

            def fast_path():
                for l in range(L):
                    if l:
                        for u in range(RING):
                            pool.wait_ge(s_store[u], 16 * GROUPS * l)

                    def gather(b, u, used):
                        g = l * NB + b
                        if used:
                            pool.wait_ge(s_glo, g - RING + 1)
                            pool.nop(nofuse=True)
                        nc.gpsimd.tensor_copy(idx[:, :, u:u + 1], edge_src[:, :, bass.ds(b, 1)]).then_inc(s_idx, 1)
                        pool.wait_ge(s_idx, g + 1)
                        pool.nop(nofuse=True)
                        for j in range(TILES):
                            pool.indirect_dma_start(
                                out=gath[:, u, j, :], out_offset=None, in_=states[l],
                                in_offset=bass.IndirectOffsetOnAxis(ap=idx[:, j, u:u + 1], axis=0),
                                bounds_check=last_node, oob_is_err=False).then_inc(s_gath[u], 16)

                    def split_gathered(b, u):
                        pool.wait_ge(s_ghi, l * NB + b + 1)
                        nc.gpsimd.tensor_tensor(g_lo[:, u, :, :], gath[:, u, :, :], g_hi[:, u, :, :].bitcast(F32),
                                                ALU.subtract).then_inc(s_glo, 1)

                    def step(i, u, first, last):
                        if first:
                            gather(0, 0, l > 0)
                            for v in range(3):
                                gather(v + 1, v + 1, l > 0)
                                split_gathered(v, v)
                                if v < 2:
                                    split_h(l, v, v)
                        if exists(i, u, RING - 1):
                            nb, nu, ni = after(i, u, RING - 1)
                            gather(nb, nu, l > 0 or not isinstance(ni, int) or ni > 0)
                        if exists(i, u, 2):
                            split_h(l, *after(i, u, 2)[:2])
                        if exists(i, u, 3):
                            split_gathered(*after(i, u, 3)[:2])
                        if l == L - 1 and exists_before(i, u, NLAG):
                            root(*after(i, u, -NLAG)[:2])

                    blocks(pool, step)
                    if l == L - 1:
                        for k in range(NLAG, 0, -1):
                            root(*after(GROUPS, 0, -k)[:2])

            def general_path():
                for l in range(L):
                    def edge_row(r, first):
                        k = l * NCH + r
                        pool.wait_ge(s_eld[l], 2 * 16 * (r + 1))
                        pool.nop(nofuse=True)
                        for frm, at, to in ((states[l], e_src, e_rows), (edge_sum, e_dst, e_old)):
                            pool.indirect_dma_start(out=to[:, :], out_offset=None, in_=frm,
                                                    in_offset=bass.IndirectOffsetOnAxis(ap=at[:, :], axis=0),
                                                    bounds_check=last_node, oob_is_err=False).then_inc(s_ego[l], 16)
                        pool.wait_ge(s_ev, 5 * (k + 1))
                        pool.nop(nofuse=True)
                        pool.indirect_dma_start(out=edge_sum, in_=e_new[:, :], in_offset=None,
                                                out_offset=bass.IndirectOffsetOnAxis(ap=e_at[:, :], axis=0),
                                                bounds_check=last_node, oob_is_err=False).then_inc(s_esc, 16)

                    edge_row(0, True)
                    with pool.Fori(1, NCH) as r:
                        edge_row(r, False)

                    def one(b, first):
                        split_h(l, b, 0)
                        if l == L - 1:
                            root(b, 0)

                    one_by_one(pool, one)

            pool.wait_ge(s_v, V_FLAG)
            flag = pool.value_load(flag_i[0:1, 0:1])
            with pool.If(flag == 0):
                fast_path()
            with pool.Else():
                general_path()

        @block.tensor
        def _(pe):
            pe.wait_ge(s_const, 5)
            pe.wait_ge(s_v, V_DIAG)
            for m in range(CPR):
                c = m * P
                last = nc.tensor.matmul(pA[0:NB, c:c + EP], ones[0:EP, 0:NB], diag[0:EP, m, 0:EP], start=True, stop=True)
            last.then_inc(s_bc, 1)
            pe.wait_ge(s_w, 5 * 16)
            for l in range(L):
                nc.tensor.transpose(pH[:, l * D:(l + 1) * D], w_in[:, l, :], ident[:, :])
            for c in range(3):
                nc.tensor.transpose(pO[:, c * D:(c + 1) * D], wih_in[:, c, :], ident[:, :])
            for c in range(3):
                last = nc.tensor.transpose(pR[:, c * D:(c + 1) * D], whh_in[:, c, :], ident[:, :])
            last.then_inc(s_wt, 1)
            pe.wait_ge(s_wtc, 3)
            for l, bank in enumerate((pZ, pHN, pIN, pH)):
                nc.tensor.matmul(bank[:, 0:3 * D], wT[:, l, :], wihT[:, :], start=True, stop=True).then_inc(s_wf, 1)
            pe.wait_ge(s_v, V_SLOTS)
            for j in range(TILES):
                nc.tensor.transpose(pA[:, j * NB:(j + 1) * NB], slot_dl[0:NB, j * P:(j + 1) * P], ident[0:NB, 0:NB])
            for j in range(TILES):
                last = nc.tensor.transpose(pA[:, (TILES + j) * NB:(TILES + j + 1) * NB],
                                           slot_src[0:NB, j * P:(j + 1) * P], ident[0:NB, 0:NB])
            last.then_inc(s_tab, 1)
            pe.wait_ge(s_v, V_CHECKS)
            pe.wait_ge(s_wfc, L)
            nc.tensor.matmul(pR[0:1, 0:1], checks[0:NB, :], ones[0:NB, 0:1], start=True, stop=True).then_inc(s_flag, 1)

            def at_least(s, value, start):
                if not start:
                    pe.wait_ge(s, value)

            def turn_h(l, b, u, loads, start):
                g = l * NB + b
                pe.wait_ge(s_load[u], 16 * loads)
                at_least(s_hhi, g, start)
                for k in range(RPP):
                    last = nc.tensor.transpose(pH[:, k * ROWS:(k + 1) * ROWS], h_rows[:, u, k * D:(k + 1) * D],
                                               ident[0:ROWS, 0:ROWS])
                last.then_inc(s_pH, 1)

            def sum_edges(l, b, u, start):
                g = l * NB + b
                pe.wait_ge(s_glo, g + 1)
                pe.wait_ge(s_sel, TILES * (g + 1))
                if u == 0:
                    if not start:
                        pe.wait_ge(s_alo if l == L - 1 else s_agg, g)
                elif not (isinstance(b, int) and g < 2):
                    pe.wait_ge(s_alo if l == L - 1 else s_agg, g - 1)
                sums = edge_bank(u)
                passes = [(of_rows(sums, j), part[:, u, j, :], selection(u, j))
                          for j in range(TILES) for part in (g_hi, g_lo)]
                if l == L - 1:
                    pe.wait_ge(s_hlo, g + 1)
                    passes += [(sums, ident_r[:, :], part[:, u, :]) for part in (h_hi, h_lo)]
                for k, (to, rows, columns) in enumerate(passes):
                    last = nc.tensor.matmul(to, rows, columns, start=k == 0, stop=k == len(passes) - 1)
                last.then_inc(s_pA, 1)

            def gates(l, b, u, start):
                g = l * NB + b
                pe.wait_ge(s_hlo, g + 1)
                pe.wait_ge(s_alo, g + 1)

                def product(bank, c, sides):
                    passes = []
                    for side in sides:
                        x_hi, x_lo, w_hi, w_lo = {
                            "in": (a_hi, a_lo, wf_hi[:, l, c * D:(c + 1) * D], wf_lo[:, l, c * D:(c + 1) * D]),
                            "state": (h_hi, h_lo, whh_hi[:, c * D:(c + 1) * D], whh_lo[:, c * D:(c + 1) * D])}[side]
                        passes += [(w_hi, x_hi), (w_hi, x_lo), (w_lo, x_hi)]
                    for k, (w, xx) in enumerate(passes):
                        last = nc.tensor.matmul(bank[:, 0:BLK], w, xx[:, u, :], start=k == 0, stop=k == len(passes) - 1)
                    return last

                at_least(s_r, g, start)
                product(pR, 0, ("in", "state")).then_inc(s_R, 1)
                at_least(s_t1, g, start)
                product(pHN, 2, ("state",)).then_inc(s_HN, 1)
                at_least(s_t2, g, start)
                product(pIN, 2, ("in",)).then_inc(s_IN, 1)
                at_least(s_z, g, start)
                product(pZ, 1, ("in", "state")).then_inc(s_Z, 1)

            def turn_back(l, b, u, start):
                g = l * NB + b
                pe.wait_ge(s_new, g + 1)
                if l == L - 1:
                    if start:
                        pe.wait_ge(s_o, l * NB)
                    else:
                        pe.wait_ge(s_y, b)
                else:
                    at_least(s_o, g, start and l == 0)
                for k in range(RPP):
                    last = nc.tensor.transpose(pO[0:ROWS, k * D:(k + 1) * D], newT[:, u, k * ROWS:(k + 1) * ROWS],
                                               ident[:, :])
                last.then_inc(s_pO, 1)

            def fast_path():
                for l in range(L):
                    def step(i, u, first, last):
                        start = first and l == 0
                        if first:
                            turn_h(l, 0, 0, GROUPS * l + 1, start)
                            turn_h(l, 1, 1, GROUPS * l + 1, False)
                            sum_edges(l, 0, 0, start)
                            if l < L - 1:
                                sum_edges(l, 1, 1, False)
                        if exists(i, u, 2):
                            nb, nu, ni = after(i, u, 2)
                            turn_h(l, nb, nu, GROUPS * l + ni + 1, False)
                        if l == L - 1 and not last:
                            sum_edges(l, *after(i, u)[:2], False)
                        gates(l, RING * i + u, u, start)
                        if l < L - 1 and exists(i, u, 2):
                            sum_edges(l, *after(i, u, 2)[:2], False)
                        if not first:
                            pb, pu, _ = after(i, u, -1)
                            turn_back(l, pb, pu, isinstance(i, int) and pb == 0)
                        if last:
                            turn_back(l, RING * i + u, u, False)

                    blocks(pe, step)

            def general_path():
                for l in range(L):
                    def edge_row(r, first):
                        k = l * NCH + r
                        pe.wait_ge(s_ediag, k + 1)
                        nc.tensor.matmul(pZ[0:CHUNK, 0:CHUNK], ones[0:CHUNK, 0:CHUNK], e_diag[:, :],
                                         start=True, stop=True).then_inc(s_ebc, 1)
                        pe.wait_ge(s_ev, 5 * k + 2)
                        pe.wait_ge(s_ego[l], 2 * 16 * (r + 1))
                        nc.tensor.matmul(pHN[0:CHUNK, 0:D], e_same[:, :], e_rows[:, :],
                                         start=True, stop=True).then_inc(s_esum, 1)

                    edge_row(0, True)
                    with pe.Fori(1, NCH) as r:
                        edge_row(r, False)

                    def one(b, first):
                        start = first and l == 0
                        turn_h(l, b, 0, l * NB + b + 1, start)
                        pe.wait_ge(s_agld, 16 * (l * NB + b + 1))
                        at_least(s_agg, l * NB + b, start)
                        for k in range(RPP):
                            last = nc.tensor.transpose(pA[:, k * ROWS:(k + 1) * ROWS], y_rows[:, 1, k * D:(k + 1) * D],
                                                       ident[0:ROWS, 0:ROWS])
                        last.then_inc(s_pA, 1)
                        gates(l, b, 0, start)
                        turn_back(l, b, 0, first)

                    one_by_one(pe, one)

            pe.wait_ge(s_v, V_FLAG)
            flag = pe.value_load(flag_i[0:1, 0:1])
            with pe.If(flag == 0):
                fast_path()
            with pe.Else():
                general_path()

        @block.scalar
        def _(act):
            act.wait_ge(s_const, 5)
            nc.scalar.copy(ident_r[:, :], ident[:, :]).then_inc(s_identr, 1)
            act.wait_ge(s_wt, 1)
            nc.scalar.copy(wT[:, :, :].rearrange("p l d -> p (l d)"), pH[:, 0:L * D]).then_inc(s_wtc, 1)
            nc.scalar.copy(wihT[:, :], pO[:, 0:3 * D]).then_inc(s_wtc, 1)
            nc.scalar.copy(whh_hi[:, :], pR[:, 0:3 * D]).then_inc(s_wtc, 1)
            for l, bank in enumerate((pZ, pHN, pIN, pH)):
                act.wait_ge(s_wf, l + 1)
                nc.scalar.copy(wf_hi[:, l, :], bank[:, 0:3 * D]).then_inc(s_wfc, 1)

            def copy_h(l, b, u):
                act.wait_ge(s_pH, l * NB + b + 1)
                nc.scalar.copy(hT[:, u, :], pH[:, 0:BLK]).then_inc(s_hT, 1)
                nc.scalar.copy(h_hi[:, u, :], pH[:, 0:BLK]).then_inc(s_hhi, 1)

            def high_gathered(l, b, u, gathers):
                act.wait_ge(s_gath[u], 16 * TILES * gathers)
                nc.scalar.copy(g_hi[:, u, :, :].rearrange("p j d -> p (j d)"),
                               gath[:, u, :, :].rearrange("p j d -> p (j d)")).then_inc(s_ghi, 1)

            def high_part(l, b, u, summed=False):
                act.wait_ge(s_pA if summed else s_agg, l * NB + b + 1)
                nc.scalar.copy(a_hi[:, u, :], edge_bank(u) if summed else aggT[:, u, :]).then_inc(s_ahi, 1)

            def r_gate(l, b, u):
                act.wait_ge(s_R, l * NB + b + 1)
                nc.scalar.activation(rg[:, :], pR[:, 0:BLK], ACT.Sigmoid, bias=bsum[:, 0:1]).then_inc(s_r, 1)

            def n_and_z(l, b, u):
                g = l * NB + b
                act.wait_ge(s_t2, g + 1)
                nc.scalar.activation(ng[:, :], t2[:, :], ACT.Tanh, bias=bih[:, 2:3]).then_inc(s_n, 1)
                act.wait_ge(s_Z, g + 1)
                nc.scalar.activation(zg[:, :], pZ[:, 0:BLK], ACT.Sigmoid, bias=bsum[:, 1:2]).then_inc(s_z, 1)

            def rows_out(l, b, u, stored):
                g = l * NB + b
                if stored is not None:
                    act.wait_ge(s_store[u], 16 * stored)
                if l < L - 1:
                    act.wait_ge(s_pO, g + 1)
                    nc.scalar.copy(o_rows[:, u, :], pO[0:ROWS, 0:RPP * D]).then_inc(s_o, 1)
                else:
                    act.wait_ge(s_nmr, b + 1)
                    for k in range(RPP):
                        last = nc.scalar.activation(o_rows[:, u, k * D:(k + 1) * D], y_rows[:, u, k * D:(k + 1) * D],
                                                    ACT.Identity, bias=nmr[:, u, k:k + 1], scale=rstd[:, u, k:k + 1])
                    last.then_inc(s_o, 1)

            def fast_path():
                for l in range(L):
                    lag = NLAG + 1 if l == L - 1 else 2

                    def earlier(i):
                        return None if l == 0 and isinstance(i, int) and i == 0 else GROUPS * l + i

                    def step(i, u, first, last):
                        if first:
                            copy_h(l, 0, 0)
                            copy_h(l, 1, 1)
                            high_gathered(l, 0, 0, GROUPS * l + 1)
                            high_part(l, 0, 0, l == L - 1)
                            high_gathered(l, 1, 1, GROUPS * l + 1)
                            high_gathered(l, 2, 2, GROUPS * l + 1)

                        def rows():
                            if exists_before(i, u, lag):
                                pb, pu, pi = after(i, u, -lag)
                                rows_out(l, pb, pu, earlier(pi))

                        def high():
                            if not last:
                                high_part(l, *after(i, u)[:2], l == L - 1)

                        if l < L - 1:
                            high()
                        r_gate(l, RING * i + u, u)
                        if l < L - 1:
                            rows()
                        if exists(i, u, 2):
                            copy_h(l, *after(i, u, 2)[:2])
                        if l == L - 1:
                            high()
                        if exists(i, u, 3):
                            nb, nu, ni = after(i, u, 3)
                            high_gathered(l, nb, nu, GROUPS * l + ni + 1)
                        n_and_z(l, RING * i + u, u)
                        if l == L - 1:
                            rows()

                    blocks(act, step)
                    for k in range(lag, 0, -1):
                        pb, pu, pi = after(GROUPS, 0, -k)
                        rows_out(l, pb, pu, earlier(pi))

            def general_path():
                for l in range(L):
                    def one(b, first):
                        copy_h(l, b, 0)
                        high_part(l, b, 0)
                        r_gate(l, b, 0)
                        n_and_z(l, b, 0)
                        rows_out(l, b, 0, None if first and l == 0 else l * NB + b)

                    one_by_one(act, one)

            act.wait_ge(s_v, V_FLAG)
            flag = act.value_load(flag_i[0:1, 0:1])
            with act.If(flag == 0):
                fast_path()
            with act.Else():
                general_path()

        @block.vector
        def _(dve):
            steps = [0]

            def done(ins):
                steps[0] += 1
                ins.then_inc(s_v, 1)
                dve.wait_ge(s_v, steps[0])

            v = nc.vector
            n_ = slice(0, NB)
            dve.wait_ge(s_edges, 4 * 16)
            dve.wait_ge(s_const, 5)
            firsts = dst_i[0:EP, :].rearrange("p (m j) -> p m j", j=CHUNK)[:, :, 0]
            done(v.tensor_copy(stat[0:EP, 0:CPR], firsts))
            for m in range(CPR):
                last = v.tensor_scalar(diag[0:EP, m, 0:EP], ident[0:EP, 0:EP], stat[0:EP, m:m + 1], None, ALU.mult)
            done(last)
            assert steps[0] == V_DIAG
            done(v.tensor_tensor(tmp_a[0:EP, 0:EC], nxt_i[0:EP, :], dst_i[0:EP, :], ALU.subtract))
            done(v.tensor_tensor(tmp_b[0:EP, 0:EC], src_i[0:EP, :], dst_i[0:EP, :], ALU.not_equal))
            done(v.scalar_tensor_tensor(tmp_c[0:EP, 0:EC], tmp_a[0:EP, 0:EC], 1.0, tmp_b[0:EP, 0:EC],
                                        ALU.is_equal, ALU.mult, accum_out=sums[0:EP, 0:1]))
            done(v.tensor_scalar(tmp_c[0:EP, 0:EC], tmp_a[0:EP, 0:EC], 0.0, None, ALU.is_equal, ALU.add,
                                 accum_out=sums[0:EP, 1:2]))
            done(v.tensor_scalar(tmp_c[0:EP, 0:EC], tmp_a[0:EP, 0:EC], 1.0, None, ALU.is_equal, ALU.add,
                                 accum_out=sums[0:EP, 2:3]))
            dve.wait_ge(s_bc, 1)
            bc = pA[n_, 0:CPR * P].rearrange("p (m q) -> p m q", q=P)[:, :, 0:EP]
            done(v.tensor_scalar(tmp_c[n_, 0:CPR * EP].rearrange("p (m q) -> p m q", q=EP), bc, blk_start[n_, :], None,
                                 ALU.is_lt, ALU.add, accum_out=stat[n_, 5:6]))
            done(v.tensor_scalar(stat[n_, 6:7], stat[n_, 5:6], -1.0, 0.0, ALU.add, ALU.max))
            for m in range(WCH):
                last = v.tensor_scalar(chunk_i[n_, m:m + 1], stat[n_, 6:7], float(m), None, ALU.add)
            done(last)
            assert steps[0] == V_ROWS
            dve.wait_ge(s_win, WCH * 16)
            done(v.tensor_copy(winf[n_, :], win_dst[n_, :]))
            done(v.tensor_tensor(tmp_b[n_, :], winf[n_, 0:WIN], winf[n_, 1:WIN + 1], ALU.is_equal))
            done(v.tensor_scalar(tmp_a[n_, :], winf[n_, 0:WIN], blk_start[n_, :], None, ALU.subtract))
            done(v.scalar_tensor_tensor(tmp_c[n_, :], tmp_a[n_, :], 0.0, tmp_b[n_, :], ALU.is_ge, ALU.mult))
            done(v.scalar_tensor_tensor(tmp_b[n_, :], tmp_a[n_, :], float(BLK), tmp_c[n_, :], ALU.is_lt, ALU.mult,
                                        accum_out=sums[n_, 3:4]))
            done(v.tensor_scalar(dl_i[n_, :], tmp_a[n_, :], 0.0, float(BLK - 1), ALU.max, ALU.min))
            done(v.tensor_scalar(key_i[n_, :], dl_i[n_, :], 16, 1 << 30, ALU.logical_shift_left, ALU.bitwise_or))
            dve.wait_ge(s_w, 5 * 16)
            done(v.tensor_tensor(bsum[:, :], bih[:, :], bhh[:, :], ALU.add))
            assert steps[0] == V_BIAS
            dve.wait_ge(s_wtc, 3)
            v.tensor_tensor(whh_lo[:, :], pR[:, 0:3 * D], whh_hi[:, :].bitcast(F32), ALU.subtract)
            dve.wait_ge(s_wfc, L)
            for l, bank in enumerate((pZ, pHN, pIN, pH)):
                last = v.tensor_tensor(wf_lo[:, l, :], bank[:, 0:3 * D], wf_hi[:, l, :].bitcast(F32), ALU.subtract)
            done(last)
            assert steps[0] == V_WEIGHTS
            dve.wait_ge(s_winsrc, WCH * 16)
            done(v.tensor_tensor(dl_i[n_, :], key_i[n_, :], win_src[n_, :], ALU.bitwise_or))
            done(v.tensor_tensor(tmp_a[n_, :], dl_i[n_, :].bitcast(F32), tmp_b[n_, :], ALU.mult))
            cur, nxt = tmp_a, tmp_c
            width = LIVE
            for r in range(CAP // 8):
                done(v.max(keys[n_, 8 * r:8 * r + 8], cur[n_, 0:width]))
                if r < CAP // 8 - 1:
                    width -= SHRINK
                    done(v.match_replace(nxt[n_, 0:width], keys[n_, 8 * r:8 * r + 8], cur[n_, 0:width], 0.0))
                    cur, nxt = nxt, cur
            done(v.tensor_scalar(tmp_b[n_, 0:CAP], keys[n_, :], 0.0, None, ALU.is_gt, ALU.add, accum_out=sums[n_, 4:5]))
            ki = keys[n_, :].bitcast(I32)
            v.tensor_scalar(slot_dl_i[n_, :], ki, 16, None, ALU.logical_shift_right)
            v.tensor_scalar(slot_ok_i[n_, :], ki, 30, None, ALU.logical_shift_right)
            done(v.tensor_scalar(slot_src_i[n_, :], ki, 0xFFFF, None, ALU.bitwise_and))
            v.tensor_scalar(slot_dl[n_, :], slot_dl_i[n_, :], -16384.0, None, ALU.add)
            done(v.tensor_scalar(tmp_b[n_, 0:CAP], slot_ok_i[n_, :], -65536.0, 65536.0, ALU.mult, ALU.add))
            done(v.tensor_tensor(slot_src[n_, :], tmp_b[n_, 0:CAP], slot_src_i[n_, :], ALU.add))
            assert steps[0] == V_SLOTS
            dve.wait_ge(s_tab, 1)
            v.tensor_copy(edge_dl[:, :, :].rearrange("p j b -> p (j b)"), pA[:, 0:TILES * NB])
            done(v.tensor_copy(edge_src[:, :, :].rearrange("p j b -> p (j b)"), pA[:, TILES * NB:2 * TILES * NB]))
            assert steps[0] == V_TABLES
            done(v.tensor_tensor(checks[n_, :], sums[n_, 0:1], sums[n_, 1:2], ALU.subtract))
            done(v.scalar_tensor_tensor(checks[n_, :], checks[n_, :], float(EC), sums[n_, 2:3], ALU.add, ALU.subtract))
            done(v.scalar_tensor_tensor(checks[n_, :], sums[n_, 3:4], sums[n_, 4:5], checks[n_, :],
                                        ALU.not_equal, ALU.add))
            for j in range(1, TILES):
                done(v.scalar_tensor_tensor(checks[n_, :], slot_dl[n_, j * P:j * P + 1], float(RPP * ENDS[j]),
                                            checks[n_, :], ALU.is_ge, ALU.add))
            assert steps[0] == V_CHECKS
            dve.wait_ge(s_flag, 1)
            done(v.tensor_tensor(flag_i[0:1, 0:1], pR[0:1, 0:1], dst_i[0:1, 0:1], ALU.add))
            assert steps[0] == V_FLAG

            def select(b, u, j):
                v.tensor_scalar(selection(u, j), of_rows(node_of_col[:, :], j), edge_dl[:, j, bass.ds(b, 1)],
                                None, ALU.is_equal).then_inc(s_sel, 1)

            def low_part(l, b, u, summed=False):
                dve.wait_ge(s_ahi, l * NB + b + 1)
                if summed:
                    dve.wait_ge(s_pA, l * NB + b + 1)
                v.tensor_tensor(a_lo[:, u, :], edge_bank(u) if summed else aggT[:, u, :], a_hi[:, u, :].bitcast(F32),
                                ALU.subtract).then_inc(s_alo, 1)

            def aggregate(l, b, u):
                g = l * NB + b
                dve.wait_ge(s_hT, g + 1)
                dve.wait_ge(s_pA, g + 1)
                v.tensor_tensor(aggT[:, u, :], edge_bank(u), hT[:, u, :], ALU.add).then_inc(s_agg, 1)

            def r_times_hn(l, b, u, start):
                g = l * NB + b
                if not start:
                    dve.wait_ge(s_e, g)
                dve.wait_ge(s_HN, g + 1)
                dve.wait_ge(s_r, g + 1)
                v.scalar_tensor_tensor(t1[:, :], pHN[:, 0:BLK], bhh[:, 2:3], rg[:, :],
                                       ALU.add, ALU.mult).then_inc(s_t1, 1)

            def n_argument(l, b, u, start):
                g = l * NB + b
                if not start:
                    dve.wait_ge(s_new, g)
                dve.wait_ge(s_IN, g + 1)
                dve.wait_ge(s_t1, g + 1)
                v.tensor_tensor(t2[:, :], pIN[:, 0:BLK], t1[:, :], ALU.add).then_inc(s_t2, 1)

            def difference(l, b, u):
                dve.wait_ge(s_n, l * NB + b + 1)
                v.tensor_tensor(t1[:, :], hT[:, u, :], ng[:, :], ALU.subtract).then_inc(s_d, 1)

            def product(l, b, u):
                g = l * NB + b
                dve.wait_ge(s_z, g + 1)
                dve.wait_ge(s_d, g + 1)
                v.tensor_tensor(t2[:, :], zg[:, :], t1[:, :], ALU.mult).then_inc(s_e, 1)

            def new_state(l, b, u):
                g = l * NB + b
                dve.wait_ge(s_e, g + 1)
                v.tensor_tensor(newT[:, u, :], t2[:, :], ng[:, :], ALU.add).then_inc(s_new, 1)

            def residual(b, u, loaded):
                dve.wait_ge(s_pO, (L - 1) * NB + b + 1)
                dve.wait_ge(s_xld[u], 16 * (loaded + 1))
                v.scalar_tensor_tensor(y_rows[:, u, :], x_rows[:, u, :], 2.0, pO[0:ROWS, 0:RPP * D],
                                       ALU.mult, ALU.add).then_inc(s_y, 1)

            def row_stats(b, u, _):
                dve.wait_ge(s_y, b + 1)
                for k in range(RPP):
                    last = v.bn_stats(bn[:, u, k, :], y_rows[:, u, k * D:(k + 1) * D])
                last.then_inc(s_bn, 1)

            def moments(b, u, _):
                dve.wait_ge(s_bn, b + 1)
                v.tensor_tensor(mv[:, u, :, 0], bn[:, u, :, 1], bn[:, u, :, 4], ALU.add)
                v.scalar_tensor_tensor(mv[:, u, :, 1], bn[:, u, :, 2], D * EPS, bn[:, u, :, 5], ALU.add, ALU.add)
                v.tensor_tensor(mv[:, u, :, 2], bn[:, u, :, 1], bn[:, u, :, 4], ALU.subtract).then_inc(s_mv, 1)

            def squared_difference(b, u, _):
                dve.wait_ge(s_mv, 2 * b + 1)
                v.scalar_tensor_tensor(mv[:, u, :, 3], mv[:, u, :, 2], 0.25, mv[:, u, :, 2],
                                       ALU.mult, ALU.mult).then_inc(s_mv, 1)

            def variance(b, u, _):
                dve.wait_ge(s_mv, 2 * b + 2)
                v.scalar_tensor_tensor(veps[:, u, :], mv[:, u, :, 1], 1.0 / D, mv[:, u, :, 3],
                                       ALU.mult, ALU.add).then_inc(s_eps, 1)

            def shift(b, u, _):
                dve.wait_ge(s_rstd, b + 1)
                v.scalar_tensor_tensor(nmr[:, u, :], mv[:, u, :, 0], -0.5, rstd[:, u, :],
                                       ALU.mult, ALU.mult).then_inc(s_nmr, 1)

            def fast_path():
                for l in range(L):
                    def step(i, u, first, last):
                        if first:
                            for early in range(3):
                                for j in range(TILES):
                                    select(early, early, j)
                            if l < L - 1:
                                aggregate(l, 0, 0)
                            low_part(l, 0, 0, l == L - 1)

                        def select_later(j):
                            if exists(i, u, 3):
                                select(*after(i, u, 3)[:2], j)

                        def of_last(work):
                            if not first:
                                work(l, *after(i, u, -1)[:2])

                        def on_rows(work, lag):
                            if l == L - 1 and exists_before(i, u, lag):
                                pb, pu, pi = after(i, u, -lag)
                                work(pb, pu, pi)

                        if l < L - 1 and not last:
                            aggregate(l, *after(i, u)[:2])
                        of_last(difference)
                        on_rows(residual, NLAG - 1)
                        on_rows(moments, NLAG)
                        of_last(product)
                        on_rows(squared_difference, NLAG)
                        if l < L - 1 and not last:
                            low_part(l, *after(i, u)[:2])
                        r_times_hn(l, RING * i + u, u, first and l == 0)
                        of_last(new_state)
                        on_rows(variance, NLAG)
                        select_later(1)
                        n_argument(l, RING * i + u, u, first and l == 0)
                        if l == L - 1 and not last:
                            low_part(l, *after(i, u)[:2], True)
                        on_rows(shift, NLAG + 1)
                        on_rows(row_stats, NLAG - 1)
                        select_later(0)
                        if last:
                            for work in (difference, product, new_state):
                                work(l, RING * i + u, u)

                    blocks(dve, step)
                    if l == L - 1:
                        for k in range(NLAG + 1, 0, -1):
                            pb, pu, pi = after(GROUPS, 0, -k)
                            if k < NLAG:
                                residual(pb, pu, pi)
                                row_stats(pb, pu, pi)
                            if k <= NLAG:
                                for work in (moments, squared_difference, variance):
                                    work(pb, pu, pi)
                            shift(pb, pu, pi)

            def general_path():
                dve.wait_ge(s_zero, 8)
                for l in range(L):
                    def edge_row(r, first):
                        k = l * NCH + r
                        dve.wait_ge(s_eld[l], 2 * 16 * (r + 1))
                        v.tensor_copy(e_dstf[:, :], e_dst[:, :]).then_inc(s_ev, 1)
                        dve.wait_ge(s_ev, 5 * k + 1)
                        v.tensor_scalar(e_diag[:, :], ident[0:CHUNK, 0:CHUNK], e_dstf[:, :], None,
                                        ALU.mult).then_inc(s_ediag, 1)
                        dve.wait_ge(s_ebc, k + 1)
                        v.tensor_scalar(e_same[:, :], pZ[0:CHUNK, 0:CHUNK], e_dstf[:, :], None,
                                        ALU.is_equal).then_inc(s_ev, 1)
                        dve.wait_ge(s_ev, 5 * k + 2)
                        v.scalar_tensor_tensor(e_junk[:, :], e_same[:, :], 1.0, before[:, :], ALU.mult, ALU.mult,
                                               accum_out=e_dup[:, :]).then_inc(s_ev, 1)
                        dve.wait_ge(s_ev, 5 * k + 3)
                        v.scalar_tensor_tensor(e_at[:, :], e_dup[:, :], 65536.0, e_dstf[:, :],
                                               ALU.mult, ALU.add).then_inc(s_ev, 1)
                        dve.wait_ge(s_esum, k + 1)
                        v.tensor_tensor(e_new[:, :], pHN[0:CHUNK, 0:D], e_old[:, :], ALU.add).then_inc(s_ev, 1)

                    edge_row(0, True)
                    with dve.Fori(1, NCH) as r:
                        edge_row(r, False)

                    def one(b, first):
                        dve.wait_ge(s_pA, l * NB + b + 1)
                        v.tensor_copy(aggT[:, 0, :], pA[:, 0:BLK]).then_inc(s_agg, 1)
                        low_part(l, b, 0)
                        start = first and l == 0
                        r_times_hn(l, b, 0, start)
                        n_argument(l, b, 0, start)
                        for work in (difference, product, new_state):
                            work(l, b, 0)
                        if l == L - 1:
                            for work in (residual, row_stats, moments, squared_difference, variance, shift):
                                work(b, 0, b)

                    one_by_one(dve, one)

            flag = dve.value_load(flag_i[0:1, 0:1])
            with dve.If(flag == 0):
                fast_path()
            with dve.Else():
                general_path()


_INS = ['x', 'src', 'dst', 'L0_gnn_weight', 'L0_gnn_w_ih', 'L0_gnn_w_hh', 'L0_gnn_b_ih', 'L0_gnn_b_hh']
_OUTS = [((50000, 128), 'float32')]


def kernel(**inputs):
    import numpy as _np
    import concourse.bacc as _bacc
    from concourse import mybir as _mybir
    from concourse.bass_utils import run_bass_kernel_spmd as _run

    nc = _bacc.Bacc("TRN2", target_bir_lowering=False, num_devices=1)
    arrays, args = {}, []
    for name in _INS:
        a = _np.ascontiguousarray(inputs[name])
        arrays[f"in_{name}_dram"] = a
        args.append(nc.dram_tensor(f"in_{name}_dram", a.shape, _mybir.dt.from_np(a.dtype), kind="ExternalInput").ap())
    for i, (shape, dtype) in enumerate(_OUTS):
        dt = _mybir.dt.from_np(_np.dtype(dtype))
        args.append(nc.dram_tensor(f"out_{i}_dram", shape, dt, kind="ExternalOutput").ap())
    build(nc, *args)
    r = _run(nc, [arrays], core_ids=[0])
    got = tuple(r.results[0][f"out_{i}_dram"] for i in range(len(_OUTS)))
    return got[0]
```
